# Optimizing a Trainium2 kernel written in Bass

```python
import numpy as np
import jax
import jax.numpy as jnp

def _softmax(x, axis=-1):
    return jax.nn.softmax(x, axis=axis)

def _gelu(x):
    return jax.nn.gelu(x, approximate=True)

def _silu(x):
    return jax.nn.silu(x)

def _sigmoid(x):
    return jax.nn.sigmoid(x)

def _layernorm(x, axis=-1, eps=1e-05):
    m = jnp.mean(x, axis=axis, keepdims=True)
    v = jnp.var(x, axis=axis, keepdims=True)
    return (x - m) / jnp.sqrt(v + eps)

def _scatter_add(tgt, idx, src, axis=0):
    return tgt.at[idx].add(src)

def _segment_sum(src, seg, n):
    return jax.ops.segment_sum(src, seg, n)
kernel_name = 'mk_vit_tower_d1_tok_img1024_r4_7b8331'

def setup_inputs(seed: int=0):
    np.random.seed(seed)
    _w = jnp.asarray

    def _rec_inputs():
        import jax
        import jax.numpy as jnp
        _rk = jax.random.key(seed)
        x = -0.000125008 + 0.999885 * jax.random.normal(jax.random.fold_in(_rk, 1), (8, 512, 256, 4), jnp.float32)
        return x
    x = _rec_inputs()

    def _L0_tok_setup():
        import jax, jax.numpy as jnp
        import numpy as np
        key = jax.random.key(seed)
        k1, k2, k3 = jax.random.split(key, 3)
        B, H, I, O, Dp1 = (4, 512, 256, 256, 4)
        x = jax.random.normal(k1, (B, H, I, Dp1), dtype=jnp.float32)
        weight = 0.1 * jax.random.normal(k2, (O, Dp1), dtype=jnp.float32)
        weighted_sum = 0.1 * jax.random.normal(k3, (O, I), dtype=jnp.float32)
        return {'x': x, 'weight': weight, 'weighted_sum': weighted_sum}
    _L0_tok_all = _L0_tok_setup()
    _L0_tok_in = {k: v for k, v in _L0_tok_all.items() if k in ('weight', 'weighted_sum')}
    del _L0_tok_all

    def _L0_attn_setup():
        import jax, jax.numpy as jnp
        import numpy as np
        B, S, D = (2, 512, 256)
        H = 16
        HD = D // H
        SCALE = HD ** (-0.5)
        EPS = 1e-12

        def _rope_sin_cos(length, half, dtype):
            positions = jnp.arange(length, dtype=dtype)
            freqs = jnp.arange(half, dtype=dtype)
            inv_freq = 1.0 / 2500 ** (freqs / max(1, half))
            theta = jnp.einsum('s,f->sf', positions, inv_freq)
            return (jnp.sin(theta)[None, None], jnp.cos(theta)[None, None])

        def _rotate(x, sin, cos):
            x_even = x[..., 0::2]
            x_odd = x[..., 1::2]
            r_even = x_even * cos - x_odd * sin
            r_odd = x_even * sin + x_odd * cos
            return jnp.stack([r_even, r_odd], axis=-1).reshape(x.shape)
        key = jax.random.key(seed)
        k1, k2, k3 = jax.random.split(key, 3)
        tokens = jax.random.normal(k1, (B, S, D), dtype=jnp.float32)
        qkv_w = jax.random.normal(k2, (3 * D, D), dtype=jnp.float32) * D ** (-0.5)
        qkv_b = jnp.zeros((3 * D,), dtype=jnp.float32)
        out_w = jax.random.normal(k3, (D, D), dtype=jnp.float32) * D ** (-0.5)
        out_b = jnp.zeros((D,), dtype=jnp.float32)
        return {'tokens': tokens, 'qkv_w': qkv_w, 'qkv_b': qkv_b, 'out_w': out_w, 'out_b': out_b}
    _L0_attn_all = _L0_attn_setup()
    _L0_attn_in = {k: v for k, v in _L0_attn_all.items() if k in ('qkv_w', 'qkv_b', 'out_w', 'out_b')}
    del _L0_attn_all

    def _L0_ffn_setup():
        import jax, jax.numpy as jnp
        import numpy as np
        B, S, D, H, E = (4, 512, 256, 1024, 8)
        THRESHOLD = 0.5
        key = jax.random.key(seed)
        ks = jax.random.split(key, 7)
        s_in = 1.0 / np.sqrt(D)
        s_h = 1.0 / np.sqrt(H)
        return {'x': jax.random.normal(ks[0], (B, S, D), dtype=jnp.float32), 'Wg': jax.random.uniform(ks[1], (D, E), jnp.float32, -s_in, s_in), 'bg': jax.random.uniform(ks[2], (E,), jnp.float32, -s_in, s_in), 'W1': jax.random.uniform(ks[3], (E, D, H), jnp.float32, -s_in, s_in), 'b1': jax.random.uniform(ks[4], (E, H), jnp.float32, -s_in, s_in), 'W2': jax.random.uniform(ks[5], (E, H, D), jnp.float32, -s_h, s_h), 'b2': jax.random.uniform(ks[6], (E, D), jnp.float32, -s_h, s_h)}
    _L0_ffn_all = _L0_ffn_setup()
    _L0_ffn_in = {k: v for k, v in _L0_ffn_all.items() if k in ('Wg', 'bg', 'W1', 'b1', 'W2', 'b2')}
    del _L0_ffn_all
    return {'x': x, 'L0_tok_weight': _L0_tok_in['weight'], 'L0_tok_weighted_sum': _L0_tok_in['weighted_sum'], 'L0_attn_qkv_w': _L0_attn_in['qkv_w'], 'L0_attn_qkv_b': _L0_attn_in['qkv_b'], 'L0_attn_out_w': _L0_attn_in['out_w'], 'L0_attn_out_b': _L0_attn_in['out_b'], 'L0_ffn_Wg': _L0_ffn_in['Wg'], 'L0_ffn_bg': _L0_ffn_in['bg'], 'L0_ffn_W1': _L0_ffn_in['W1'], 'L0_ffn_b1': _L0_ffn_in['b1'], 'L0_ffn_W2': _L0_ffn_in['W2'], 'L0_ffn_b2': _L0_ffn_in['b2']}

def reference(x, L0_tok_weight, L0_tok_weighted_sum, L0_attn_qkv_w, L0_attn_qkv_b, L0_attn_out_w, L0_attn_out_b, L0_ffn_Wg, L0_ffn_bg, L0_ffn_W1, L0_ffn_b1, L0_ffn_W2, L0_ffn_b2):
    import jax
    import jax.numpy as jnp

    def _L0_tok_ref(x, weight, weighted_sum):
        import jax, jax.numpy as jnp
        import numpy as np
        return jnp.einsum('bhid,oi,od->bho', x, weighted_sum, weight)

    def _L0_attn_ref(tokens, qkv_w, qkv_b, out_w, out_b):
        import jax, jax.numpy as jnp
        import numpy as np
        B, S, D = (2, 512, 256)
        H = 16
        HD = D // H
        SCALE = HD ** (-0.5)
        EPS = 1e-12

        def _rope_sin_cos(length, half, dtype):
            positions = jnp.arange(length, dtype=dtype)
            freqs = jnp.arange(half, dtype=dtype)
            inv_freq = 1.0 / 2500 ** (freqs / max(1, half))
            theta = jnp.einsum('s,f->sf', positions, inv_freq)
            return (jnp.sin(theta)[None, None], jnp.cos(theta)[None, None])

        def _rotate(x, sin, cos):
            x_even = x[..., 0::2]
            x_odd = x[..., 1::2]
            r_even = x_even * cos - x_odd * sin
            r_odd = x_even * sin + x_odd * cos
            return jnp.stack([r_even, r_odd], axis=-1).reshape(x.shape)
        batch, length, _ = tokens.shape
        qkv = tokens @ qkv_w.T + qkv_b
        qkv = qkv.reshape(batch, length, 3, H, HD)
        qkv = jnp.transpose(qkv, (0, 3, 1, 2, 4))
        q, k, v = (qkv[..., 0, :], qkv[..., 1, :], qkv[..., 2, :])
        sin, cos = _rope_sin_cos(length, HD // 2, q.dtype)
        q = _rotate(q, sin, cos)
        k = _rotate(k, sin, cos)
        q = q / jnp.maximum(jnp.linalg.norm(q, axis=-1, keepdims=True), EPS)
        k = k / jnp.maximum(jnp.linalg.norm(k, axis=-1, keepdims=True), EPS)
        scores = jnp.einsum('bhqd,bhkd->bhqk', q, k) * SCALE
        attn = jax.nn.softmax(scores, axis=-1)
        out = jnp.einsum('bhqk,bhkd->bhqd', attn, v)
        out = jnp.transpose(out, (0, 2, 1, 3)).reshape(batch, length, D)
        return out @ out_w.T + out_b

    def _L0_ffn_ref(x, Wg, bg, W1, b1, W2, b2):
        import jax, jax.numpy as jnp
        import numpy as np
        B, S, D, H, E = (4, 512, 256, 1024, 8)
        THRESHOLD = 0.5
        b, s, d = x.shape
        x_flat = x.reshape(-1, d)
        probs = jax.nn.sigmoid(x_flat @ Wg + bg)
        mask = (probs > THRESHOLD).astype(x_flat.dtype)
        weights = probs * mask
        h = jax.nn.relu(jnp.einsum('td,edh->eth', x_flat, W1) + b1[:, None, :])
        expert_out = jnp.einsum('eth,ehd->etd', h, W2) + b2[:, None, :]
        combined = jnp.einsum('te,etd->td', weights, expert_out)
        return combined.reshape(b, s, d)
    h = _L0_tok_ref(x, L0_tok_weight, L0_tok_weighted_sum)
    h = h + _L0_attn_ref(_layernorm(h, axis=-1), L0_attn_qkv_w, L0_attn_qkv_b, L0_attn_out_w, L0_attn_out_b)
    h = h + _L0_ffn_ref(_layernorm(h, axis=-1), L0_ffn_Wg, L0_ffn_bg, L0_ffn_W1, L0_ffn_b1, L0_ffn_W2, L0_ffn_b2)
    return h

_drawn_inputs = setup_inputs


def setup_inputs(seed=0):
    import zlib

    import numpy as np

    out = dict(_drawn_inputs(seed))
    spreads = {'L0_attn_qkv_b': (0.0, 0.1), 'L0_attn_out_b': (0.0, 0.1)}
    factors = {}
    for name, (base, spread) in spreads.items():
        noise = np.random.default_rng([zlib.crc32(name.encode()), seed]).standard_normal(out[name].shape)
        drawn = base * np.exp(spread * noise) if base else spread * noise
        out[name] = jnp.asarray(drawn.astype(out[name].dtype))
    for name, factor in factors.items():
        out[name] = (out[name] * factor).astype(out[name].dtype)
    return out
```

```python
from contextlib import ExitStack

import concourse.bass as bass
from concourse import mybir

F32 = mybir.dt.float32
F32R = mybir.dt.float32r
F16 = mybir.dt.float16
I32 = mybir.dt.int32
ALU = mybir.AluOpType
ACT = mybir.ActivationFunctionType
AX = mybir.AxisListType

P = 128
BATCHES = 8
TOKENS = 512
TT = TOKENS // P
D = 256
DK = D // P
TAPS = 4
XK = D * TAPS // P
HEADS = 16
HD = D // HEADS
GROUPS = HEADS // 4
QKV = 3 * D
EXPERTS = 8
HIDDEN = 1024
HM = HIDDEN // P
CHUNKS = EXPERTS * HM
LAG = 2
HBUFS = 4
UNITS = GROUPS * TT
LN_EPS = 1e-5
NORM_EPS = 1e-12
SCORE_SCALE = HD ** -0.5
ONE_BITS = 127 << 23
EXPONENT = 0x7F800000
RSQRT_GUESS = 0x5F3759DF
TOP = 2.0 ** 14
FLOOR = 2.0 ** -40


def merged_order():
    attention = []
    for t in range(TT):
        attention += [(1 + t, "mix", t), (6 + t, "ln1_turn", t), (7 + t, "qkv", t),
                      (13 + t, "qk_turn", t), (54 + t, "att_turn", t), (55 + t, "project", t)]
    for u in range(UNITS):
        attention += [(18 + 2 * u, "scores", u), (19 + 2 * u, "weigh", u)]
    for g in range(GROUPS):
        attention.append((18 + 2 * (4 * g + 4) + 1, "out_turn", g))
    attention += [(5, "ln1", 0), (11.5, "qk_norm", 0), (59, "ln2", 0)]
    for t in range(TT):
        attention.append((59.5 + t, "ln2_turn", t))
    attention.append((63.8, "gate", 0))
    attention.sort(key=lambda s: s[0])
    return attention


def bodies():
    attention = [(s, n) for _, s, n in merged_order()]
    experts, merged = [], []
    waiting = merged_order()
    for c in range(CHUNKS + LAG):
        if c < CHUNKS:
            experts.append(("f1", c))
            merged.append(("f1", c))
        if c == CHUNKS:
            while waiting:
                merged.append(waiting.pop(0)[1:])
            merged.append(("hand_x", 0))
        while waiting and waiting[0][0] < c + 1:
            merged.append(waiting.pop(0)[1:])
        if c >= LAG:
            for order in (experts, merged):
                order.append(("f2", c - LAG))
                if (c - LAG) % HM == HM - 1:
                    order.append(("acc", (c - LAG) // HM))
    merged.append(("hand_acc", 0))
    first = []
    prep = [("prep", e) for e in range(EXPERTS)]
    for k, s in enumerate(attention):
        first.append(s)
        if k % 6 == 5 and prep:
            first.append(prep.pop(0))
    first += prep + [("hand_x", 0), ("hand_acc", 0)]
    return first, merged, experts


class Signal:

    def __init__(self, sem, per_batch):
        self.sem, self.per_batch = sem, per_batch

    def at(self, batch, count):
        return batch * self.per_batch + count


def wait(eng, signal, batch, count):
    value = signal.at(batch, count)
    if not (isinstance(value, int) and value <= 0):
        eng.wait_ge(signal.sem, value)


class Chain:

    def __init__(self, sem):
        self.sem, self.per_batch, self.count = sem, None, 0

    def start(self, batch):
        if self.count:
            self.per_batch = self.count
        self.batch, self.count = batch, 0

    def link(self, eng, ins):
        ins.then_inc(self.sem, 1)
        self.count += 1
        base = 0 if self.per_batch is None else self.batch * self.per_batch
        eng.wait_ge(self.sem, base + self.count)


def build(nc, x_t, mix_w, mix_sum_t, qkv_w_t, qkv_b, out_w_t, out_b, gate_w, gate_b, w1, b1_t, w2, b2,
          rope_cos, rope_sin, unit, out):
    first_order, merged, last_order = bodies()
    w1_parts = nc.dram_tensor("w1_parts", [EXPERTS, P, 2, DK, HIDDEN], F16, kind="Internal").ap()
    w2_parts = nc.dram_tensor("w2_parts", [EXPERTS, P, 2, HM, D], F16, kind="Internal").ap()

    with ExitStack() as ctx:
        def sb(name, shape, dt=F32):
            return ctx.enter_context(nc.sbuf_tensor(name, shape, dt))

        def bank(name):
            return ctx.enter_context(nc.psum_tensor(name, [P, 512], F32))

        def sem(name):
            return ctx.enter_context(nc.semaphore(name))

        def signal(name, per_batch):
            return Signal(sem(name), per_batch)

        ident = sb("ident", [P, P])
        ident16 = sb("ident16", [P, P], F16)
        ones = sb("ones", [P, 1])
        mix = sb("mix", [P, 2, XK, D], F32R)
        qkvw = sb("qkvw", [P, 2, DK, QKV], F32R)
        outw = sb("outw", [P, 2, DK, D], F32R)
        qkvb = sb("qkvb", [P, QKV])
        outb = sb("outb", [P, D])
        gatew = sb("gatew", [P, DK, EXPERTS])
        gateb = sb("gateb", [P, EXPERTS])
        b2sb = sb("b2sb", [EXPERTS, D])
        b1raw = sb("b1raw", [P, EXPERTS, HM])
        b1s = sb("b1s", [P, EXPERTS, HM])
        cos = sb("cos", [P, TT, HD])
        sin = sb("sin", [P, TT, HD])
        unscale = sb("unscale", [P, EXPERTS])

        raw = sb("raw", [P, 4096])
        w1s = [sb(f"w1s{i}", [P, 2, DK, HIDDEN], F16) for i in range(2)]
        w2s = [sb(f"w2s{i}", [P, 2, HM, D], F16) for i in range(2)]
        xraw = [sb(f"xraw{i}", [P, XK, P]) for i in range(2)]

        xh = sb("xh", [P, XK, P], F32R)
        xl = sb("xl", [P, XK, P], F32R)
        resid = sb("resid", [P, TT, D])
        normed = sb("normed", [P, TT, D])
        turned_h = sb("turned_h", [P, DK, P], F32R)
        turned_l = sb("turned_l", [P, DK, P], F32R)
        qk = sb("qk", [P, TT, 2 * D])
        tmp_a = sb("tmp_a", [P, 2 * D])
        tmp_b = sb("tmp_b", [P, 2 * D])
        stack = sb("stack", [P, 2, HEADS, 4, HD], F16)
        qt = sb("qt", [P, HEADS // 2, TOKENS], F16)
        kt = sb("kt", [P, HEADS // 2, TOKENS], F16)
        v1 = sb("v1", [P, TT, HEADS, 2, HD])
        probs = [sb(f"probs{i}", [P, 4, TOKENS]) for i in range(2)]
        osb = tmp_b
        att = normed
        stats = sb("stats", [P, TT, 2, 3])
        mean = sb("mean", [P, TT])
        var = sb("var", [P, TT])
        gap = sb("gap", [P, TT])
        ss = sb("ss", [P, TT, 2 * HEADS])
        y1 = sb("y1", [P, TT * 2 * HEADS])
        y2 = sb("y2", [P, TT * 2 * HEADS])
        y3 = sb("y3", [P, TT * 2 * HEADS])
        rc = sb("rc", [P, TT, 4])
        wide = sb("wide", [P, DK, P])
        lg = sb("lg", [P, TT, EXPERTS])
        eg = sb("eg", [P, TT, EXPERTS])
        pg = sb("pg", [P, TT, EXPERTS])
        wg = sb("wg", [P, TT, EXPERTS])
        wt = sb("wt", [EXPERTS, TOKENS])
        x16n = sb("x16n", [P, 2, DK, TOKENS], F16)
        x16 = sb("x16", [P, 2, DK, TOKENS], F16)
        gwn = sb("gwn", [P, TT, EXPERTS])
        gw = sb("gw", [P, TT, EXPERTS])
        accn = sb("accn", [P, TT, D])
        acc = sb("acc", [P, TT, D])
        h32 = [sb(f"h32_{i}", [P, TOKENS]) for i in range(2)]
        hh = [sb(f"hh{i}", [P, TOKENS], F16) for i in range(HBUFS)]
        hl = [sb(f"hl{i}", [P, TOKENS], F16) for i in range(HBUFS)]
        mx = sb("mx", [P, 3])
        mxr = sb("mxr", [P, 3])
        bound = sb("bound", [P, 2])
        pow2 = sb("pow2", [P, 2])
        inv2 = sb("inv2", [P, 2])
        scl = sb("scl", [P, 2])

        bank_s = [bank(f"bank_s{i}") for i in range(2)]
        bank_m = bank("bank_m")
        bank_o = bank("bank_o")
        bank_h = [bank(f"bank_h{i}") for i in range(2)]
        bank_f = [bank(f"bank_f{i}") for i in range(2)]
        turn_ps = bank_m[:, :].rearrange("p (k t) -> p k t", t=P)

        consts_in = sem("consts_in")
        raw_in = sem("raw_in")
        raw_used = sem("raw_used")
        set_v = Chain(sem("set_v"))
        set_hi = sem("set_hi")
        weights_ready = sem("weights_ready")
        maxima = sem("maxima")
        maxima_all = sem("maxima_all")
        scales = sem("scales")
        parts_hi = sem("parts_hi")
        parts_lo = sem("parts_lo")
        parts_out = [sem(f"parts_out{i}") for i in range(2)]
        w1_in = [signal(f"w1_in{i}", 16 * EXPERTS // 2) for i in range(2)]
        w2_in = [signal(f"w2_in{i}", 16 * EXPERTS // 2) for i in range(2)]
        x_in = [signal(f"x_in{i}", 16 * TT // 2) for i in range(2)]
        x_hi = signal("x_hi", TT)
        x_lo = signal("x_lo", TT)
        mixed = signal("mixed", TT)
        mixed_out = signal("mixed_out", 2 * TT)
        ln1_out = signal("ln1_out", TT)
        ln1_turned = signal("ln1_turned", TT)
        ln1_hi = signal("ln1_hi", TT)
        ln1_lo = signal("ln1_lo", TT)
        resid_biased = signal("resid_biased", 1)
        qkv_done = signal("qkv_done", TT)
        qkv_out = signal("qkv_out", 2 * TT)
        qk_unit = signal("qk_unit", TT)
        stack_hi = signal("stack_hi", TT)
        stack_ready = signal("stack_ready", 2 * TT)
        stack_turned = signal("stack_turned", TT)
        qt_out = signal("qt_out", TT)
        kt_out = signal("kt_out", TT)
        scored = signal("scored", 4 * UNITS)
        exped = signal("exped", 4 * UNITS)
        weighed = signal("weighed", UNITS)
        o_out = signal("o_out", GROUPS)
        o_turned = signal("o_turned", GROUPS)
        att_out = signal("att_out", GROUPS)
        att_turned = signal("att_turned", TT)
        att_hi = signal("att_hi", TT)
        att_lo = signal("att_lo", TT)
        projected = signal("projected", TT)
        h2_out = signal("h2_out", TT)
        ln2_out = signal("ln2_out", TT)
        ln2_turned = signal("ln2_turned", TT)
        ln2_wide = signal("ln2_wide", 2 * TT)
        ln2_lo = signal("ln2_lo", TT)
        gated = signal("gated", TT)
        logit = signal("logit", 1)
        gexp = signal("gexp", 1)
        gweight = signal("gweight", 1)
        gturned = signal("gturned", 1)
        gt_out = signal("gt_out", 1)
        b2_done = signal("b2_done", 2)
        att_v = Chain(sem("att_v"))
        accn_ready = signal("accn_ready", 2)
        handed_x = signal("handed_x", 1)
        handed_acc = signal("handed_acc", 2)
        z_ready = signal("z_ready", CHUNKS)
        h_hi = signal("h_hi", 2 * CHUNKS)
        h_lo = signal("h_lo", CHUNKS)
        f2_done = signal("f2_done", CHUNKS)
        acc_done = signal("acc_done", EXPERTS * TT)
        stored = signal("stored", 16)

        block = ctx.enter_context(nc.Block())

        def run(eng, steps):
            for stage, n in first_order:
                steps(stage, n, None, 0)
            for stage, n in merged:
                steps(stage, n, 0, 1)
            with eng.Fori(1, BATCHES - 1) as i:
                for stage, n in merged:
                    steps(stage, n, i, i + 1)
            for stage, n in last_order:
                steps(stage, n, BATCHES - 1, None)

        @block.sync
        def _(sp):
            for dst, src in ((ident, unit), (gatew, gate_w.rearrange("(k p) e -> p k e", p=P)), (b1raw, b1_t),
                             (cos, rope_cos), (sin, rope_sin), (b2sb, b2),
                             (qkvb, qkv_b.partition_broadcast(P)), (outb, out_b.partition_broadcast(P)),
                             (gateb, gate_b.partition_broadcast(P))):
                sp.dma_start(dst[:], src).then_inc(consts_in, 16)
            taps = raw[:, 0:TAPS * D].rearrange("p (t o) -> p t o", t=TAPS)
            sums = raw[:, TAPS * D:(TAPS + DK) * D].rearrange("p (k o) -> p k o", k=DK)
            sp.dma_start(taps, mix_w.partition_broadcast(P)).then_inc(raw_in, 16)
            sp.dma_start(sums, mix_sum_t.rearrange("(k p) o -> p k o", p=P)).then_inc(raw_in, 16)
            sp.wait_ge(raw_used, 2)
            sp.dma_start(raw[:, 0:DK * QKV].rearrange("p (k n) -> p k n", k=DK),
                         qkv_w_t.rearrange("(k p) n -> p k n", p=P)).then_inc(raw_in, 16)
            sp.dma_start(raw[:, DK * QKV:DK * (QKV + D)].rearrange("p (k n) -> p k n", k=DK),
                         out_w_t.rearrange("(k p) n -> p k n", p=P)).then_inc(raw_in, 16)

            def load_x(b):
                for t in range(TT):
                    wait(sp, x_lo, b, t - 1)
                    wait(sp, x_hi, b, t - 1)
                    sp.dma_start(xraw[t % 2][:], x_t[b * TT + t]).then_inc(x_in[t % 2].sem, 16)

            def load_expert(b, e):
                s = e % 2
                wait(sp, z_ready, b, HM * (e - 1))
                sp.dma_start(w1s[s][:], w1_parts[e]).then_inc(w1_in[s].sem, 16)
                wait(sp, f2_done, b, HM * (e - 1))
                sp.dma_start(w2s[s][:], w2_parts[e]).then_inc(w2_in[s].sem, 16)

            def store(b):
                wait(sp, acc_done, b, EXPERTS * TT)
                sp.dma_start(out[b].rearrange("(t p) d -> p t d", p=P), acc[:]).then_inc(stored.sem, 16)

            load_x(0)
            for e in range(EXPERTS):
                sp.wait_ge(raw_used, 4 + 2 * e)
                sp.dma_start(raw[:, 0:2048].rearrange("p (k n) -> p k n", k=DK),
                             w1[e].rearrange("(k p) n -> p k n", p=P)).then_inc(raw_in, 16)
                sp.dma_start(raw[:, 2048:4096].rearrange("p (k n) -> p k n", k=HM),
                             w2[e].rearrange("(k p) n -> p k n", p=P)).then_inc(raw_in, 16)
                if e:
                    sp.wait_ge(parts_lo, 2 * e)
                    sp.wait_ge(parts_hi, 2 * e)
                    sp.dma_start(w1_parts[e - 1], w1s[(e - 1) % 2][:]).then_inc(parts_out[(e - 1) % 2], 16)
                    sp.dma_start(w2_parts[e - 1], w2s[(e - 1) % 2][:]).then_inc(parts_out[(e - 1) % 2], 16)
            sp.wait_ge(parts_lo, 2 * EXPERTS)
            sp.wait_ge(parts_hi, 2 * EXPERTS)
            sp.dma_start(w1_parts[EXPERTS - 1], w1s[1][:]).then_inc(parts_out[1], 16)
            sp.dma_start(w2_parts[EXPERTS - 1], w2s[1][:]).then_inc(parts_out[1], 16)
            for done in parts_out:
                sp.wait_ge(done, 32 * EXPERTS // 2)
            load_expert(0, 0)
            load_expert(0, 1)

            def body(b, more):
                if more:
                    load_x(b + 1)
                for e in range(2, EXPERTS):
                    load_expert(b, e)
                if more:
                    load_expert(b + 1, 0)
                    load_expert(b + 1, 1)
                store(b)

            body(0, True)
            with sp.Fori(1, BATCHES - 1) as i:
                body(i, True)
            body(BATCHES - 1, False)
            sp.wait_ge(stored.sem, 16 * BATCHES)

        @block.gpsimd
        def _(pool):
            def steps(stage, n, fb, ab):
                if stage == "prep":
                    pool.wait_ge(maxima, 3 * (n + 1))
                    if n:
                        pool.wait_ge(scales, n)
                    pool.partition_all_reduce(mxr[:], mx[:], P, bass.bass_isa.ReduceOp.max).then_inc(maxima_all, 1)
                elif stage == "qkv" and n == TT - 1:
                    wait(pool, ln1_out, ab, TT)
                    pool.tensor_tensor(resid[:], resid[:], outb[:].unsqueeze(1).broadcast_to([P, TT, D]),
                                       ALU.add).then_inc(resid_biased.sem, 1)

            pool.wait_ge(consts_in, 16 * 9)
            run(pool, steps)

        @block.scalar
        def _(act):
            def copy(out_ap, in_ap):
                return act.activation(out_ap, in_ap, ACT.Copy)

            act.wait_ge(set_v.sem, 1 + XK // DK * DK)
            copy(mix[:, 0].rearrange("p k o -> p (k o)"),
                 probs[0][:].rearrange("p j t -> p (j t)")).then_inc(set_hi, 1)
            act.wait_ge(raw_in, 64)
            copy(qkvw[:, 0].rearrange("p k n -> p (k n)"), raw[:, 0:DK * QKV]).then_inc(set_hi, 1)
            copy(outw[:, 0].rearrange("p k n -> p (k n)"),
                 raw[:, DK * QKV:DK * (QKV + D)]).then_inc(set_hi, 1)

            def split_x(b, t):
                wait(act, x_in[t % 2], b, 16 * (t // 2 + 1))
                wait(act, mixed, b, t)
                copy(xh[:], xraw[t % 2][:]).then_inc(x_hi.sem, 1)

            def steps(stage, n, fb, ab):
                if stage == "mix":
                    split_x(ab, n)
                elif stage == "ln1_turn":
                    wait(act, ln1_turned, ab, n + 1)
                    wait(act, qkv_done, ab, n)
                    wait(act, projected, ab, 0)
                    copy(turned_h[:], turn_ps[:, 0:DK, :]).then_inc(ln1_hi.sem, 1)
                elif stage == "qk_turn":
                    wait(act, qk_unit, ab, n + 1)
                    wait(act, stack_turned, ab, n)
                    copy(stack[:, :, :, 0, :], tmp_a[:].rearrange("p (a h d) -> p a h d", a=2, d=HD))\
                        .then_inc(stack_hi.sem, 1)
                    wait(act, stack_turned, ab, n + 1)
                    wait(act, scored, ab, 0)
                    copy(qt[:, :, n * P:(n + 1) * P],
                         bank_s[0][:, :].bitcast(F16).rearrange("p (h t) -> p h t", t=P)).then_inc(qt_out.sem, 1)
                elif stage == "scores":
                    for j in range(4):
                        wait(act, scored, ab, 4 * n + j + 1)
                        if j == 0:
                            wait(act, weighed, ab, n - 1)
                        act.activation(probs[n % 2][:, j, :], bank_s[j % 2][:, :], ACT.Exp,
                                       scale=SCORE_SCALE).then_inc(exped.sem, 1)
                elif stage == "out_turn":
                    wait(act, weighed, ab, 4 * (n + 1))
                    wait(act, o_turned, ab, n)
                    copy(osb[:], bank_o[:, :]).then_inc(o_out.sem, 1)
                elif stage == "att_turn":
                    wait(act, att_turned, ab, n + 1)
                    wait(act, projected, ab, n)
                    wait(act, qkv_done, ab, TT)
                    copy(turned_h[:], turn_ps[:, 0:DK, :]).then_inc(att_hi.sem, 1)
                elif stage == "ln2_turn":
                    wait(act, ln2_turned, ab, n + 1)
                    wait(act, gated, ab, n)
                    wait(act, ln2_lo, ab, n)
                    copy(wide[:], turn_ps[:, 0:DK, :]).then_inc(ln2_wide.sem, 1)
                    wait(act, handed_x, ab, 0)
                    copy(x16n[:, 0, :, n * P:(n + 1) * P], turn_ps[:, 0:DK, :]).then_inc(ln2_wide.sem, 1)
                elif stage == "gate":
                    wait(act, logit, ab, 1)
                    act.activation(eg[:], lg[:], ACT.Exp, scale=-1.0).then_inc(gexp.sem, 1)
                    wait(act, gturned, ab, 1)
                    copy(wt[:, :], bank_m[0:EXPERTS, :]).then_inc(gt_out.sem, 1)
                elif stage == "f1":
                    e, m = divmod(n, HM)
                    wait(act, z_ready, fb, n + 1)
                    wait(act, h_lo, fb, n - 1)
                    act.activation(h32[n % 2][:], bank_h[n % 2][:, :], ACT.Relu,
                                   bias=b1s[:, e, m:m + 1]).then_inc(h_hi.sem, 1)
                    wait(act, f2_done, fb, n - HBUFS + 1)
                    act.activation(hh[n % HBUFS][:], bank_h[n % 2][:, :], ACT.Relu,
                                   bias=b1s[:, e, m:m + 1]).then_inc(h_hi.sem, 1)
                elif stage == "prep":
                    s = n % 2
                    act.wait_ge(scales, n + 1)
                    if n >= 2:
                        act.wait_ge(parts_out[s], 32 * (n // 2))
                    act.activation(w1s[s][:, 0].rearrange("p k n -> p (k n)"), raw[:, 0:2048], ACT.Copy,
                                   scale=scl[:, 0:1]).then_inc(parts_hi, 1)
                    act.activation(w2s[s][:, 0].rearrange("p k n -> p (k n)"), raw[:, 2048:4096], ACT.Copy,
                                   scale=scl[:, 1:2]).then_inc(parts_hi, 1)

            run(act, steps)

        @block.tensor
        def _(pe):
            def parts(out_ap, high, low, w, lo_w, start=True, stop=True):
                n = len(high)
                for k in range(n):
                    pe.matmul(out_ap, high[k], w[k], start=start and k == 0, stop=False, skip_group_check=True)
                    pe.matmul(out_ap, high[k], lo_w[k], start=False, stop=False, skip_group_check=True)
                    last = pe.matmul(out_ap, low[k], w[k], start=False, stop=stop and k == n - 1,
                                     skip_group_check=True)
                return last

            def turn(signal_, source):
                for k in range(DK):
                    last = pe.transpose(turn_ps[:, k, :], source(k), ident[:])
                last.then_inc(signal_.sem, 1)

            def steps(stage, n, fb, ab):
                if stage == "mix":
                    wait(pe, x_hi, ab, n + 1)
                    wait(pe, x_lo, ab, n + 1)
                    wait(pe, mixed_out, ab, 2 * (n - 1))
                    if n < 2:
                        wait(pe, accn_ready, ab, 0)
                    last = parts(bank_s[n % 2][:, 0:D], [xh[:, k, :] for k in range(XK)],
                                 [xl[:, k, :] for k in range(XK)], [mix[:, 0, k, :] for k in range(XK)],
                                 [mix[:, 1, k, :] for k in range(XK)])
                    last.then_inc(mixed.sem, 1)
                elif stage == "ln1_turn":
                    wait(pe, ln1_out, ab, n + 1)
                    wait(pe, ln1_lo, ab, n)
                    if n == 0:
                        wait(pe, gt_out, ab, 0)
                    turn(ln1_turned, lambda k: normed[:, n, k * P:(k + 1) * P])
                elif stage == "qkv":
                    wait(pe, ln1_hi, ab, n + 1)
                    wait(pe, ln1_lo, ab, n + 1)
                    wait(pe, mixed_out, ab, 2 * TT)
                    wait(pe, qkv_out, ab, 2 * n)
                    high = [turned_h[:, k, :] for k in range(DK)]
                    low = [turned_l[:, k, :] for k in range(DK)]
                    parts(bank_s[0][:, :], high, low, [qkvw[:, 0, k, 0:2 * D] for k in range(DK)],
                          [qkvw[:, 1, k, 0:2 * D] for k in range(DK)])
                    last = parts(bank_s[1][:, 0:D], high, low, [qkvw[:, 0, k, 2 * D:QKV] for k in range(DK)],
                                 [qkvw[:, 1, k, 2 * D:QKV] for k in range(DK)])
                    last.then_inc(qkv_done.sem, 1)
                elif stage == "qk_turn":
                    wait(pe, stack_ready, ab, 2 * (n + 1))
                    wait(pe, qkv_out, ab, 2 * TT)
                    wait(pe, qt_out, ab, n)
                    wait(pe, kt_out, ab, n)
                    for a in range(2):
                        turned = bank_s[a][:, :].bitcast(F16).rearrange("p (h t) -> p h t", t=P)
                        for h in range(HEADS // 2):
                            last = pe.transpose(turned[:, h, :],
                                                stack[:, a, 2 * h:2 * h + 2, :, :].rearrange("p h s d -> p (h s d)"),
                                                ident16[:])
                    last.then_inc(stack_turned.sem, 1)
                elif stage == "scores":
                    g, tile = divmod(n, TT)
                    if n == 0:
                        wait(pe, qt_out, ab, TT)
                        wait(pe, kt_out, ab, TT)
                    for j in range(4):
                        h = 4 * g + j
                        lo = 64 * (h % 2)
                        wait(pe, exped, ab, 4 * n + j - 1)
                        pe.matmul(bank_s[j % 2][:, :], kt[lo:lo + 64, h // 2, tile * P:(tile + 1) * P],
                                  qt[lo:lo + 64, h // 2, :], start=True, stop=True).then_inc(scored.sem, 1)
                elif stage == "weigh":
                    g, tile = divmod(n, TT)
                    wait(pe, exped, ab, 4 * (n + 1))
                    if n == 0:
                        wait(pe, qkv_out, ab, 2 * TT)
                        wait(pe, logit, ab, 0)
                    if tile == 0:
                        wait(pe, o_out, ab, g)
                    for j in range(4):
                        h = 4 * g + j
                        last = pe.matmul(bank_o[32 * j:32 * j + 32, :],
                                         v1[:, tile, h, :, :].rearrange("p s d -> p (s d)"),
                                         probs[n % 2][:, j, :], start=(tile == 0), stop=(tile == TT - 1),
                                         skip_group_check=True)
                    last.then_inc(weighed.sem, 1)
                elif stage == "out_turn":
                    wait(pe, o_out, ab, n + 1)
                    wait(pe, att_out, ab, n)
                    wait(pe, ln1_lo, ab, TT)
                    for t in range(TT):
                        last = pe.transpose(turn_ps[:, t, :], osb[:, t * P:(t + 1) * P], ident[:])
                    last.then_inc(o_turned.sem, 1)
                elif stage == "att_turn":
                    wait(pe, att_out, ab, GROUPS)
                    wait(pe, att_lo, ab, n)
                    turn(att_turned, lambda k: att[:, n, k * P:(k + 1) * P])
                elif stage == "project":
                    wait(pe, att_hi, ab, n + 1)
                    wait(pe, att_lo, ab, n + 1)
                    wait(pe, exped, ab, 4 * UNITS)
                    wait(pe, h2_out, ab, n - 1)
                    last = parts(bank_s[n % 2][:, 0:D], [turned_h[:, k, :] for k in range(DK)],
                                 [turned_l[:, k, :] for k in range(DK)], [outw[:, 0, k, :] for k in range(DK)],
                                 [outw[:, 1, k, :] for k in range(DK)])
                    last.then_inc(projected.sem, 1)
                elif stage == "ln2_turn":
                    wait(pe, ln2_out, ab, n + 1)
                    wait(pe, att_lo, ab, TT)
                    wait(pe, ln2_wide, ab, 2 * n)
                    turn(ln2_turned, lambda k: normed[:, n, k * P:(k + 1) * P])
                    wait(pe, ln2_wide, ab, 2 * n + 1)
                    if n == 0:
                        wait(pe, o_out, ab, GROUPS)
                    for k in range(DK):
                        last = pe.matmul(bank_o[:, n * EXPERTS:(n + 1) * EXPERTS], wide[:, k, :], gatew[:, k, :],
                                         start=(k == 0), stop=(k == DK - 1), skip_group_check=True)
                    last.then_inc(gated.sem, 1)
                elif stage == "gate":
                    wait(pe, gweight, ab, 1)
                    wait(pe, ln2_wide, ab, 2 * TT)
                    for t in range(TT):
                        last = pe.transpose(bank_m[0:EXPERTS, t * P:(t + 1) * P], wg[:, t, :], ident[:])
                    last.then_inc(gturned.sem, 1)
                    wait(pe, gt_out, ab, 1)
                    wait(pe, h2_out, ab, TT)
                    for t in range(TT):
                        last = pe.matmul(bank_s[t // 2][:, t % 2 * D:(t % 2 + 1) * D], wt[:, t * P:(t + 1) * P],
                                         b2sb[:, :], start=True, stop=True, skip_group_check=True)
                        if t % 2:
                            last.then_inc(b2_done.sem, 1)
                elif stage == "f1":
                    e, m = divmod(n, HM)
                    if n == 0:
                        wait(pe, handed_x, fb, 1)
                    if m == 0:
                        wait(pe, w1_in[e % 2], fb, 16 * (e // 2 + 1))
                    wait(pe, h_hi, fb, 2 * (n - 1))
                    w = w1s[e % 2]
                    for k in range(DK):
                        for wp, xp in ((0, 0), (0, 1), (1, 0)):
                            last = pe.matmul(bank_h[n % 2][:, :], w[:, wp, k, m * P:(m + 1) * P], x16[:, xp, k, :],
                                             start=(k == 0 and wp + xp == 0), stop=(k == DK - 1 and wp == 1),
                                             skip_group_check=True)
                    last.then_inc(z_ready.sem, 1)
                elif stage == "f2":
                    e, m = divmod(n, HM)
                    wait(pe, h_lo, fb, n + 1)
                    if m == 0:
                        wait(pe, w2_in[e % 2], fb, 16 * (e // 2 + 1))
                    w = w2s[e % 2]
                    for t in range(TT):
                        if m == 0 and t % 2 == 0:
                            wait(pe, acc_done, fb, TT * (e - 1) + t + 2)
                        o = bank_f[t // 2][:, t % 2 * D:(t % 2 + 1) * D]
                        high, low = hh[n % HBUFS][:, t * P:(t + 1) * P], hl[n % HBUFS][:, t * P:(t + 1) * P]
                        pe.matmul(o, high, w[:, 0, m, :], start=(m == 0 and t % 2 == 0), stop=False,
                                  skip_group_check=True)
                        pe.matmul(o, high, w[:, 1, m, :], start=False, stop=False, skip_group_check=True)
                        last = pe.matmul(o, low, w[:, 0, m, :], start=False, stop=(m == HM - 1),
                                         skip_group_check=True)
                    last.then_inc(f2_done.sem, 1)

            pe.wait_ge(consts_in, 16 * 9)
            pe.wait_ge(weights_ready, 1)
            run(pe, steps)

        @block.vector
        def _(dve):
            dve.wait_ge(consts_in, 16 * 9)
            dve.memset(v1[:, :, :, 1, :], 1.0)
            set_v.link(dve, dve.tensor_copy(ident16[:], ident[:]))
            dve.wait_ge(raw_in, 32)
            taps = raw[:, 0:TAPS * D].rearrange("p (t o) -> p t o", t=TAPS)
            sums = raw[:, TAPS * D:(TAPS + DK) * D].rearrange("p (k o) -> p k o", k=DK)
            made = probs[0][:].rearrange("p j t -> p (j t)").rearrange("p (k o) -> p k o", o=D)
            for t in range(TAPS):
                for k in range(DK):
                    ins = dve.tensor_tensor(made[:, t * DK + k, :], sums[:, k, :], taps[:, t, :], ALU.mult)
                    set_v.link(dve, ins)
            dve.wait_ge(set_hi, 1)
            dve.tensor_tensor(mix[:, 1].rearrange("p k o -> p (k o)"), probs[0][:].rearrange("p j t -> p (j t)"),
                              mix[:, 0].rearrange("p k o -> p (k o)").bitcast(F32), ALU.subtract)\
                .then_inc(raw_used, 2)
            dve.wait_ge(raw_in, 64)
            dve.wait_ge(set_hi, 3)
            dve.tensor_tensor(qkvw[:, 1].rearrange("p k n -> p (k n)"), raw[:, 0:DK * QKV],
                              qkvw[:, 0].rearrange("p k n -> p (k n)").bitcast(F32), ALU.subtract)\
                .then_inc(raw_used, 1)
            set_v.link(dve, dve.tensor_tensor(outw[:, 1].rearrange("p k n -> p (k n)"),
                                              raw[:, DK * QKV:DK * (QKV + D)],
                                              outw[:, 0].rearrange("p k n -> p (k n)").bitcast(F32),
                                              ALU.subtract))
            dve.memset(ones[:], 1.0).then_inc(raw_used, 1)
            dve.wait_ge(raw_used, 4)
            dve.tensor_scalar(ones[:], ones[:], 1.0, None, ALU.mult).then_inc(weights_ready, 1)

            def rsqrt(v, n):
                a, b, c = y1[:, 0:n], y2[:, 0:n], y3[:, 0:n]
                att_v.link(dve, dve.tensor_scalar(b.bitcast(I32), v.bitcast(I32), 1, None,
                                                  ALU.logical_shift_right))
                att_v.link(dve, dve.tensor_scalar(a.bitcast(I32), b.bitcast(I32), -1.0, float(RSQRT_GUESS),
                                                  ALU.mult, ALU.add))
                for _ in range(4):
                    att_v.link(dve, dve.scalar_tensor_tensor(b, a, -0.5, a, ALU.mult, ALU.mult))
                    att_v.link(dve, dve.tensor_tensor(c, b, v, ALU.mult))
                    att_v.link(dve, dve.scalar_tensor_tensor(a, c, 1.5, a, ALU.add, ALU.mult))

            def norm_scale(b):
                dve.tensor_tensor(gap[:], stats[:, :, 0, 1], stats[:, :, 1, 1], ALU.subtract)
                dve.tensor_tensor(mean[:], stats[:, :, 0, 1], stats[:, :, 1, 1], ALU.add)
                att_v.link(dve, dve.tensor_tensor(var[:], stats[:, :, 0, 2], stats[:, :, 1, 2], ALU.add))
                dve.tensor_scalar(mean[:], mean[:], 0.5, None, ALU.mult)
                att_v.link(dve, dve.scalar_tensor_tensor(gap[:], gap[:], 0.25, gap[:], ALU.mult, ALU.mult))
                att_v.link(dve, dve.scalar_tensor_tensor(var[:], var[:], 1.0 / D, gap[:], ALU.mult, ALU.add))
                att_v.link(dve, dve.tensor_scalar(var[:], var[:], LN_EPS, None, ALU.add))
                rsqrt(var[:], TT)

            def steps(stage, n, fb, ab):
                if stage == "mix":
                    if n == 0:
                        att_v.start(ab)
                    wait(dve, x_hi, ab, n + 1)
                    wait(dve, mixed, ab, n)
                    wait(dve, x_in[n % 2], ab, 16 * (n // 2 + 1))
                    dve.tensor_tensor(xl[:], xraw[n % 2][:], xh[:].bitcast(F32), ALU.subtract)\
                       .then_inc(x_lo.sem, 1)
                    wait(dve, mixed, ab, n + 1)
                    dve.tensor_copy(resid[:, n, :], bank_s[n % 2][:, 0:D]).then_inc(mixed_out.sem, 1)
                    dve.bn_stats(stats[:, n].rearrange("p h s -> p (h s)"), bank_s[n % 2][:, 0:D])\
                       .then_inc(mixed_out.sem, 1)
                elif stage == "ln1":
                    wait(dve, mixed_out, ab, 2 * TT)
                    norm_scale(ab)
                    wait(dve, ln2_turned, ab, 0)
                    for t in range(TT):
                        dve.tensor_scalar(normed[:, t, :], resid[:, t, :], mean[:, t:t + 1], y1[:, t:t + 1],
                                          ALU.subtract, ALU.mult).then_inc(ln1_out.sem, 1)
                elif stage == "ln1_turn":
                    wait(dve, ln1_hi, ab, n + 1)
                    wait(dve, qkv_done, ab, n)
                    dve.tensor_tensor(turned_l[:], turn_ps[:, 0:DK, :], turned_h[:].bitcast(F32), ALU.subtract)\
                       .then_inc(ln1_lo.sem, 1)
                elif stage == "qkv":
                    wait(dve, qkv_done, ab, n + 1)
                    if n == 0:
                        wait(dve, weighed, ab, 0)
                    att_v.link(dve, dve.tensor_tensor(qk[:, n, :], bank_s[0][:, :], qkvb[:, 0:2 * D], ALU.add))
                    dve.tensor_tensor(v1[:, n, :, 0, :], bank_s[1][:, 0:D].rearrange("p (h d) -> p h d", d=HD),
                                      qkvb[:, 2 * D:QKV].rearrange("p (h d) -> p h d", d=HD), ALU.add)\
                       .then_inc(qkv_out.sem, 2)
                    row = qk[:, n, :]
                    att_v.link(dve, dve.tensor_tensor(tmp_a[:], row, row, ALU.mult))
                    att_v.link(dve, dve.tensor_reduce(ss[:, n, :], tmp_a[:].rearrange("p (h d) -> p h d", d=HD),
                                                      AX.X, ALU.add))
                    heads = row.rearrange("p (h d) -> p h d", d=HD)
                    c = cos[:, n, :].unsqueeze(1).broadcast_to([P, 2 * HEADS, HD])
                    dve.tensor_tensor(tmp_a[:].rearrange("p (h d) -> p h d", d=HD), heads, c, ALU.mult)
                    pairs = row.rearrange("p (h f two) -> p h f two", f=HD // 2, two=2)
                    swapped = tmp_b[:].rearrange("p (h f two) -> p h f two", f=HD // 2, two=2)
                    sines = sin[:, n, :].rearrange("p (f two) -> p f two", two=2)
                    for side in range(2):
                        s = sines[:, :, side].unsqueeze(1).broadcast_to([P, 2 * HEADS, HD // 2])
                        ins = dve.tensor_tensor(swapped[:, :, :, side], pairs[:, :, :, 1 - side], s, ALU.mult)
                    att_v.link(dve, ins)
                    att_v.link(dve, dve.tensor_tensor(row, tmp_a[:], tmp_b[:], ALU.add))
                elif stage == "qk_norm":
                    flat = ss[:].rearrange("p t h -> p (t h)")
                    att_v.link(dve, dve.tensor_scalar(flat, flat, NORM_EPS * NORM_EPS, None, ALU.max))
                    rsqrt(flat, TT * 2 * HEADS)
                elif stage == "qk_turn":
                    wait(dve, stack_hi, ab, n)
                    scale = y1[:, n * 2 * HEADS:(n + 1) * 2 * HEADS].unsqueeze(2)\
                        .broadcast_to([P, 2 * HEADS, HD])
                    dve.tensor_tensor(tmp_a[:].rearrange("p (h d) -> p h d", d=HD),
                                      qk[:, n, :].rearrange("p (h d) -> p h d", d=HD), scale, ALU.mult)\
                       .then_inc(qk_unit.sem, 1)
                    wait(dve, stack_hi, ab, n + 1)
                    wait(dve, stack_turned, ab, n)
                    both = tmp_a[:].rearrange("p (a h d) -> p a h d", a=2, d=HD)
                    wait(dve, qk_unit, ab, n + 1)
                    dve.tensor_tensor(stack[:, 0, :, 1, :], both[:, 0], stack[:, 0, :, 0, :], ALU.subtract)
                    att_v.link(dve, dve.tensor_tensor(stack[:, 1, :, 2, :], both[:, 1], stack[:, 1, :, 0, :],
                                                      ALU.subtract))
                    dve.tensor_copy(stack[:, 0, :, 2:4, :], stack[:, 0, :, 0:2, :]).then_inc(stack_ready.sem, 1)
                    for s in (0, 2):
                        ins = dve.tensor_copy(stack[:, 1, :, s + 1, :], stack[:, 1, :, s, :])
                    ins.then_inc(stack_ready.sem, 1)
                    wait(dve, stack_turned, ab, n + 1)
                    wait(dve, scored, ab, 0)
                    dve.tensor_copy(kt[:, :, n * P:(n + 1) * P],
                                    bank_s[1][:, :].bitcast(F16).rearrange("p (h t) -> p h t", t=P))\
                       .then_inc(kt_out.sem, 1)
                elif stage == "out_turn":
                    wait(dve, o_turned, ab, n + 1)
                    rows = bank_m[:, :].rearrange("p (t j d) -> p t j d", t=TT, j=4)
                    att_v.link(dve, dve.reciprocal(rc[:], rows[:, :, :, HD]))
                    if n == 0:
                        wait(dve, att_turned, ab, 0)
                    dve.tensor_tensor(att[:, :, n * 4 * HD:(n + 1) * 4 * HD].rearrange("p t (j d) -> p t j d", d=HD),
                                      rows[:, :, :, 0:HD], rc[:].unsqueeze(3).broadcast_to([P, TT, 4, HD]),
                                      ALU.mult).then_inc(att_out.sem, 1)
                elif stage == "att_turn":
                    wait(dve, att_hi, ab, n + 1)
                    wait(dve, projected, ab, n)
                    dve.tensor_tensor(turned_l[:], turn_ps[:, 0:DK, :], turned_h[:].bitcast(F32), ALU.subtract)\
                       .then_inc(att_lo.sem, 1)
                elif stage == "project":
                    wait(dve, projected, ab, n + 1)
                    wait(dve, resid_biased, ab, 1)
                    wait(dve, handed_acc, ab, 0)
                    ins = dve.tensor_tensor(accn[:, n, :], bank_s[n % 2][:, 0:D], resid[:, n, :], ALU.add)
                    ins.then_inc(h2_out.sem, 1)
                    wait(dve, h2_out, ab, n + 1)
                    att_v.link(dve, dve.bn_stats(stats[:, n].rearrange("p h s -> p (h s)"), accn[:, n, :]))
                elif stage == "ln2":
                    norm_scale(ab)
                    wait(dve, ln1_turned, ab, TT)
                    for t in range(TT):
                        dve.tensor_scalar(normed[:, t, :], accn[:, t, :], mean[:, t:t + 1], y1[:, t:t + 1],
                                          ALU.subtract, ALU.mult).then_inc(ln2_out.sem, 1)
                elif stage == "ln2_turn":
                    wait(dve, ln2_wide, ab, 2 * (n + 1))
                    cut = slice(n * P, (n + 1) * P)
                    dve.tensor_tensor(x16n[:, 1, :, cut], wide[:], x16n[:, 0, :, cut], ALU.subtract)\
                       .then_inc(ln2_lo.sem, 1)
                elif stage == "gate":
                    wait(dve, gated, ab, TT)
                    dve.tensor_tensor(lg[:], bank_o[:, 0:TT * EXPERTS].rearrange("p (t e) -> p t e", t=TT),
                                      gateb[:].unsqueeze(1).broadcast_to([P, TT, EXPERTS]), ALU.add)\
                       .then_inc(logit.sem, 1)
                    wait(dve, gexp, ab, 1)
                    att_v.link(dve, dve.tensor_scalar(pg[:], eg[:], 1.0, None, ALU.add))
                    att_v.link(dve, dve.reciprocal(pg[:], pg[:]))
                    wait(dve, gturned, ab, 0)
                    flat = [z[:].rearrange("p t e -> p (t e)") for z in (wg, lg, pg)]
                    dve.scalar_tensor_tensor(flat[0], flat[1], 0.0, flat[2], ALU.is_gt, ALU.mult)\
                       .then_inc(gweight.sem, 1)
                    wait(dve, gweight, ab, 1)
                    if isinstance(ab, int) and ab == 0:
                        dve.wait_ge(scales, EXPERTS)
                    dve.tensor_tensor(gwn[:], wg[:], unscale[:].unsqueeze(1).broadcast_to([P, TT, EXPERTS]),
                                      ALU.mult).then_inc(accn_ready.sem, 1)
                    wait(dve, b2_done, ab, 2)
                    for s in range(2):
                        cut = accn[:, 2 * s:2 * s + 2, :].rearrange("p t d -> p (t d)")
                        ins = dve.tensor_tensor(cut, bank_s[s][:, :], cut, ALU.add)
                    ins.then_inc(accn_ready.sem, 1)
                elif stage == "hand_x":
                    if fb is not None:
                        wait(dve, z_ready, fb, CHUNKS)
                    wait(dve, ln2_lo, ab, TT)
                    dve.tensor_copy(x16[:], x16n[:]).then_inc(handed_x.sem, 1)
                elif stage == "hand_acc":
                    if fb is not None:
                        wait(dve, stored, fb, 16)
                        wait(dve, acc_done, fb, EXPERTS * TT)
                    wait(dve, accn_ready, ab, 2)
                    dve.tensor_copy(gw[:], gwn[:]).then_inc(handed_acc.sem, 1)
                    dve.tensor_copy(acc[:], accn[:]).then_inc(handed_acc.sem, 1)
                elif stage == "f1":
                    wait(dve, h_hi, fb, 2 * (n + 1))
                    dve.tensor_tensor(hl[n % HBUFS][:], h32[n % 2][:], hh[n % HBUFS][:], ALU.subtract)\
                       .then_inc(h_lo.sem, 1)
                elif stage == "acc":
                    wait(dve, f2_done, fb, HM * (n + 1))
                    wait(dve, handed_acc, fb, 2)
                    wait(dve, acc_done, fb, TT * n)
                    for t in range(TT):
                        dve.scalar_tensor_tensor(acc[:, t, :], bank_f[t // 2][:, t % 2 * D:(t % 2 + 1) * D],
                                                 gw[:, t, n:n + 1], acc[:, t, :], ALU.mult, ALU.add)\
                           .then_inc(acc_done.sem, 1)
                elif stage == "prep":
                    prep(n)

            def prep(e):
                s = e % 2
                dve.wait_ge(raw_in, 64 + 32 * (e + 1))
                if e:
                    dve.wait_ge(maxima_all, e)
                dve.tensor_reduce(mx[:, 0:1], raw[:, 0:2048], AX.X, ALU.max, apply_absolute_value=True)\
                   .then_inc(maxima, 1)
                dve.tensor_reduce(mx[:, 1:2], raw[:, 2048:4096], AX.X, ALU.max, apply_absolute_value=True)\
                   .then_inc(maxima, 1)
                dve.tensor_reduce(mx[:, 2:3], b1raw[:, e, :], AX.X, ALU.max, apply_absolute_value=True)\
                   .then_inc(maxima, 1)
                dve.wait_ge(maxima_all, e + 1)
                set_v.link(dve, dve.scalar_tensor_tensor(bound[:, 0:1], mxr[:, 0:1], float(D), mxr[:, 2:3],
                                                         ALU.mult, ALU.add))
                set_v.link(dve, dve.tensor_copy(bound[:, 1:2], mxr[:, 1:2]))
                set_v.link(dve, dve.tensor_scalar(bound[:], bound[:], FLOOR, None, ALU.max))
                set_v.link(dve, dve.tensor_scalar(pow2[:].bitcast(I32), bound[:].bitcast(I32), EXPONENT, None,
                                                  ALU.bitwise_and))
                set_v.link(dve, dve.tensor_scalar(inv2[:].bitcast(I32), pow2[:].bitcast(I32), -1.0,
                                                  float(2 * ONE_BITS), ALU.mult, ALU.add))
                if e:
                    dve.wait_ge(parts_hi, 2 * e)
                set_v.link(dve, dve.tensor_scalar(scl[:], inv2[:], TOP, None, ALU.mult))
                set_v.link(dve, dve.scalar_tensor_tensor(unscale[:, e:e + 1], pow2[:, 0:1], TOP ** -2, pow2[:, 1:2],
                                                         ALU.mult, ALU.mult))
                dve.tensor_scalar(b1s[:, e, :], b1raw[:, e, :], scl[:, 0:1], None, ALU.mult).then_inc(scales, 1)
                for part, (w, cut) in enumerate(((w1s[s], raw[:, 0:2048]), (w2s[s], raw[:, 2048:4096]))):
                    dve.wait_ge(parts_hi, 2 * e + part + 1)
                    dve.scalar_tensor_tensor(w[:, 1].rearrange("p k n -> p (k n)"), cut, scl[:, part:part + 1],
                                             w[:, 0].rearrange("p k n -> p (k n)"), ALU.mult, ALU.subtract)\
                       .then_inc(parts_lo, 1)
                dve.wait_ge(parts_lo, 2 * e + 2)
                dve.tensor_scalar(ones[:], ones[:], 1.0, None, ALU.mult).then_inc(raw_used, 2)

            run(dve, steps)


_OUTS = [((8, 512, 256), "float32")]


def _rope_tables(np):
    pos = np.arange(TOKENS, dtype=np.float32)
    half = HD // 2
    inv = (np.float32(1.0) / np.power(np.float32(2500), np.arange(half, dtype=np.float32) / np.float32(half)))
    theta = (pos[:, None] * inv.astype(np.float32)[None, :]).astype(np.float32)
    s, c = np.sin(theta), np.cos(theta)
    cos = np.repeat(c, 2, axis=1)
    sin = np.stack([-s, s], axis=-1).reshape(TOKENS, HD)
    return [np.ascontiguousarray(a.reshape(TT, P, HD).transpose(1, 0, 2)).astype(np.float32) for a in (cos, sin)]


def kernel(**inputs):
    import numpy as _np
    import concourse.bacc as _bacc
    from concourse import mybir as _mybir
    from concourse.bass_utils import run_bass_kernel_spmd as _run

    i = {k: _np.asarray(v) for k, v in inputs.items()}
    x_t = i["x"].reshape(BATCHES * TT, P, DK, P, TAPS).transpose(0, 3, 4, 2, 1).reshape(BATCHES * TT, P, XK, P)
    cos, sin = _rope_tables(_np)
    laid = {
        "x_t": x_t,
        "mix_w": i["L0_tok_weight"].T,
        "mix_sum_t": i["L0_tok_weighted_sum"].T,
        "qkv_w_t": i["L0_attn_qkv_w"].T,
        "qkv_b": i["L0_attn_qkv_b"],
        "out_w_t": i["L0_attn_out_w"].T,
        "out_b": i["L0_attn_out_b"],
        "gate_w": i["L0_ffn_Wg"],
        "gate_b": i["L0_ffn_bg"],
        "w1": i["L0_ffn_W1"],
        "b1_t": i["L0_ffn_b1"].reshape(EXPERTS, HM, P).transpose(2, 0, 1),
        "w2": i["L0_ffn_W2"],
        "b2": i["L0_ffn_b2"],
        "rope_cos": cos,
        "rope_sin": sin,
        "unit": _np.eye(P, dtype=_np.float32),
    }
    nc = _bacc.Bacc("TRN2", target_bir_lowering=False, num_devices=1)
    arrays, args = {}, []
    for name, a in laid.items():
        a = _np.ascontiguousarray(a)
        arrays[f"in_{name}_dram"] = a
        args.append(nc.dram_tensor(f"in_{name}_dram", a.shape, _mybir.dt.from_np(a.dtype), kind="ExternalInput").ap())
    for n, (shape, dtype) in enumerate(_OUTS):
        dt = _mybir.dt.from_np(_np.dtype(dtype))
        args.append(nc.dram_tensor(f"out_{n}_dram", shape, dt, kind="ExternalOutput").ap())
    build(nc, *args)
    r = _run(nc, [arrays], core_ids=[0])
    got = tuple(r.results[0][f"out_{n}_dram"] for n in range(len(_OUTS)))
    return got[0]
```

```python
from contextlib import ExitStack

import concourse.bass as bass
from concourse import mybir

F32 = mybir.dt.float32
F32R = mybir.dt.float32r
F16 = mybir.dt.float16
I32 = mybir.dt.int32
ALU = mybir.AluOpType
ACT = mybir.ActivationFunctionType
AX = mybir.AxisListType

P = 128
BATCHES = 8
TOKENS = 512
TT = TOKENS // P
D = 256
DK = D // P
TAPS = 4
XK = D * TAPS // P
HEADS = 16
HD = D // HEADS
GROUPS = HEADS // 4
QKV = 3 * D
EXPERTS = 8
HIDDEN = 1024
HM = HIDDEN // P
CHUNKS = EXPERTS * HM
LAG = 2
HBUFS = 4
UNITS = GROUPS * TT
LN_EPS = 1e-5
NORM_EPS = 1e-12
SCORE_SCALE = HD ** -0.5
ONE_BITS = 127 << 23
EXPONENT = 0x7F800000
RSQRT_GUESS = 0x5F3759DF
TOP = 2.0 ** 14
FLOOR = 2.0 ** -40


def attention_order():
    steps = []
    for t in range(TT):
        steps += [(1.9 + 1.5 * t if t else 1.2, "split", t), (2 + 1.5 * t, "mix", t),
                  (8.5 + 1.5 * t, "ln1_turn", t), (9.5 + 1.5 * t, "qkv", t), (9.9 + 1.5 * t, "rotate", t),
                  (16.4 + 1.5 * t, "stack", t), (17.5 + 1.5 * t, "qk_turn", t)]
    steps[steps.index((1.9 + 1.5, "split", 1))] = (2.4, "split", 1)
    steps[steps.index((1.9 + 3.0, "split", 2))] = (3.9, "split", 2)
    steps[steps.index((1.9 + 4.5, "split", 3))] = (5.4, "split", 3)
    steps += [(7, "ln1", 0), (15.5, "qk_norm", 0)]
    first = 23.0
    for n in range(2 * UNITS):
        steps.append((first + PACE * n, "scores", n))
    for u in range(UNITS):
        steps.append((first + PACE * (2 * u + 3) + 0.1, "weigh", u))
    for g in range(GROUPS):
        steps.append((first + PACE * (8 * (g + 1) + 3) + 0.2, "out_turn", g))
    tail = first + PACE * (2 * UNITS + 4) + 1
    for t in range(TT):
        steps += [(tail + t, "att_turn", t), (tail + t + 1.1, "project", t), (tail + 7.6 + 0.8 * t, "ln2_turn", t),
                  (tail + 8.3 + 0.8 * t, "logits", t)]
    steps += [(tail + 5.2, "ln2", 0), (tail + 11.2, "gates", 0), (tail + 12.7, "gates_turn", 0),
              (tail + 13.7, "bias2", 0)]
    steps.sort(key=lambda s: s[0])
    return steps


PACE = 0.67


def bodies():
    attention = attention_order()
    prep = []
    for e in range(2, EXPERTS):
        prep += [(HM * (e - 1) + 0.7, "maxima", e), (HM * (e - 1) + 3.6, "parts1", e),
                 (HM * (e - 1) + 5.6, "parts2", e)]

    def merge(waiting, hand):
        waiting, order = sorted(waiting, key=lambda s: s[0]), []
        for c in range(CHUNKS + LAG):
            if c < CHUNKS:
                order.append(("f1", c))
                while waiting and waiting[0][0] < c + 0.5:
                    order.append(waiting.pop(0)[1:])
            else:
                while waiting:
                    order.append(waiting.pop(0)[1:])
                if hand and c == CHUNKS:
                    order.append(("hand_x", 0))
            if c >= LAG:
                order.append(("f2", c - LAG))
                if (c - LAG) % HM == HM - 1:
                    order.append(("acc", (c - LAG) // HM))
            while waiting and waiting[0][0] < c + 1:
                order.append(waiting.pop(0)[1:])
        return order + [("hand_acc", 0)] * hand

    alone = [s[1:] for s in attention]
    prepared = [(stage, e) for e in range(2) for stage in ("maxima", "parts1", "parts2")]
    first = []
    for s in alone:
        first.append(s)
        if s[0] in ("ln1_turn", "qkv") and prepared:
            first.append(prepared.pop(0))
    first += prepared + [("hand_x", 0), ("hand_acc", 0)]
    return first, merge(attention + prep, True), merge(attention, True), merge([], False)


class Signal:

    def __init__(self, sem, per_batch):
        self.sem, self.per_batch = sem, per_batch

    def at(self, batch, count):
        return batch * self.per_batch + count


def wait(eng, signal, batch, count):
    value = signal.at(batch, count)
    if not (isinstance(value, int) and value <= 0):
        eng.wait_ge(signal.sem, value)


class Chain:

    def __init__(self, sem):
        self.sem, self.per_batch, self.count = sem, None, 0

    def start(self, batch):
        if self.count:
            self.per_batch = self.count
        self.batch, self.count = batch, 0

    def link(self, eng, ins):
        ins.then_inc(self.sem, 1)
        self.count += 1
        base = 0 if self.per_batch is None else self.batch * self.per_batch
        eng.wait_ge(self.sem, base + self.count)


def build(nc, x_t, mix_w, mix_sum_t, qkv_w_t, qkv_b, out_w_t, out_b, gate_w, gate_b, w1, b1_t, w2, b2,
          rope_cos, rope_sin, unit, out):
    first_order, second_order, merged, last_order = bodies()
    w1_parts = nc.dram_tensor("w1_parts", [EXPERTS, P, 2, DK, HIDDEN], F16, kind="Internal").ap()
    w2_parts = nc.dram_tensor("w2_parts", [EXPERTS, P, 2, HM, D], F16, kind="Internal").ap()

    with ExitStack() as ctx:
        def sb(name, shape, dt=F32):
            return ctx.enter_context(nc.sbuf_tensor(name, shape, dt))

        def bank(name):
            return ctx.enter_context(nc.psum_tensor(name, [P, 512], F32))

        def sem(name):
            return ctx.enter_context(nc.semaphore(name))

        def signal(name, per_batch):
            return Signal(sem(name), per_batch)

        ident = sb("ident", [P, P])
        ident16 = sb("ident16", [P, P], F16)
        ones = sb("ones", [P, 1])
        mix = sb("mix", [P, 2, XK, D], F32R)
        qkvw = sb("qkvw", [P, 2, DK, QKV], F32R)
        outw = sb("outw", [P, 2, DK, D], F32R)
        qkvb = sb("qkvb", [P, QKV])
        outb = sb("outb", [P, D])
        gatew = sb("gatew", [P, DK, EXPERTS])
        gateb = sb("gateb", [P, EXPERTS])
        b2sb = sb("b2sb", [EXPERTS, D])
        b1raw = sb("b1raw", [P, EXPERTS, HM])
        b1s = sb("b1s", [P, EXPERTS, HM])
        cos = sb("cos", [P, TT, HD])
        sin = sb("sin", [P, TT, HD])
        unscale = sb("unscale", [P, EXPERTS])

        raw = sb("raw", [P, 4096])
        w1s = [sb(f"w1s{i}", [P, 2, DK, HIDDEN], F16) for i in range(2)]
        w2s = [sb(f"w2s{i}", [P, 2, HM, D], F16) for i in range(2)]
        xraw = [sb(f"xraw{i}", [P, XK, P]) for i in range(2)]

        xh = sb("xh", [P, XK, P], F32R)
        xl = sb("xl", [P, XK, P], F32R)
        resid = sb("resid", [P, TT, D])
        normed = sb("normed", [P, TT, D])
        turned_h = sb("turned_h", [P, DK, P], F32R)
        turned_l = sb("turned_l", [P, DK, P], F32R)
        qk = sb("qk", [P, TT, 2 * D])
        tmp_a = sb("tmp_a", [P, 2 * D])
        tmp_b = sb("tmp_b", [P, 2 * D])
        stack = sb("stack", [P, 2, HEADS, 4, HD], F16)
        qt = sb("qt", [P, HEADS // 2, TOKENS], F16)
        kt = sb("kt", [P, HEADS // 2, TOKENS], F16)
        v1 = sb("v1", [P, TT, HEADS, 2, HD])
        probs = [sb(f"probs{i}", [P, 4, TOKENS]) for i in range(2)]
        osb = tmp_b
        att = normed
        stats = sb("stats", [P, TT, 2, 3])
        mean = sb("mean", [P, TT])
        var = sb("var", [P, TT])
        gap = sb("gap", [P, TT])
        ss = sb("ss", [P, TT, 2 * HEADS])
        y1 = sb("y1", [P, TT * 2 * HEADS])
        y2 = sb("y2", [P, TT * 2 * HEADS])
        y3 = sb("y3", [P, TT * 2 * HEADS])
        rc = sb("rc", [P, TT, 4])
        wide = sb("wide", [P, DK, P])
        lg = sb("lg", [P, TT, EXPERTS])
        eg = sb("eg", [P, TT, EXPERTS])
        pg = sb("pg", [P, TT, EXPERTS])
        wg = sb("wg", [P, TT, EXPERTS])
        wt = sb("wt", [EXPERTS, TOKENS])
        x16n = sb("x16n", [P, 2, DK, TOKENS], F16)
        x16 = sb("x16", [P, 2, DK, TOKENS], F16)
        gwn = sb("gwn", [P, TT, EXPERTS])
        gw = sb("gw", [P, TT, EXPERTS])
        gs = sb("gs", [P, TT])
        accn = sb("accn", [P, TT, D])
        acc = sb("acc", [P, TT, D])
        h32 = [sb(f"h32_{i}", [P, TOKENS]) for i in range(2)]
        hh = [sb(f"hh{i}", [P, TOKENS], F16) for i in range(HBUFS)]
        hl = [sb(f"hl{i}", [P, TOKENS], F16) for i in range(HBUFS)]
        mx = sb("mx", [P, 3])
        mxr = sb("mxr", [P, 3])
        bound = sb("bound", [P, 2])
        pow2 = sb("pow2", [P, 2])
        inv2 = sb("inv2", [P, 2])
        scl = sb("scl", [P, 2])

        bank_s = [bank(f"bank_s{i}") for i in range(2)]
        bank_m = bank("bank_m")
        bank_o = bank("bank_o")
        bank_h = [bank(f"bank_h{i}") for i in range(2)]
        bank_f = [bank(f"bank_f{i}") for i in range(2)]
        turn_ps = bank_m[:, :].rearrange("p (k t) -> p k t", t=P)

        consts_in = sem("consts_in")
        raw_in = sem("raw_in")
        raw_used = sem("raw_used")
        set_v = Chain(sem("set_v"))
        set_hi = sem("set_hi")
        weights_ready = sem("weights_ready")
        maxima = sem("maxima")
        maxima_all = sem("maxima_all")
        scales = sem("scales")
        parts_hi = sem("parts_hi")
        parts_lo = sem("parts_lo")
        parts_out = [sem(f"parts_out{i}") for i in range(2)]
        w1_in = [signal(f"w1_in{i}", 16 * EXPERTS // 2) for i in range(2)]
        w2_in = [signal(f"w2_in{i}", 16 * EXPERTS // 2) for i in range(2)]
        x_in = [signal(f"x_in{i}", 16 * TT // 2) for i in range(2)]
        x_hi = signal("x_hi", TT)
        x_lo = signal("x_lo", TT)
        mixed = signal("mixed", TT)
        mixed_out = signal("mixed_out", 2 * TT)
        ln1_out = signal("ln1_out", TT)
        ln1_turned = signal("ln1_turned", TT)
        ln1_hi = signal("ln1_hi", TT)
        ln1_lo = signal("ln1_lo", TT)
        resid_biased = signal("resid_biased", 1)
        qkv_done = signal("qkv_done", TT)
        qkv_out = signal("qkv_out", 2 * TT)
        qk_unit = signal("qk_unit", TT)
        stack_hi = signal("stack_hi", TT)
        stack_ready = signal("stack_ready", 2 * TT)
        stack_turned = signal("stack_turned", TT)
        qt_out = signal("qt_out", TT)
        kt_out = signal("kt_out", TT)
        scored = signal("scored", 4 * UNITS)
        exped = signal("exped", 4 * UNITS)
        weighed = signal("weighed", UNITS)
        o_out = signal("o_out", GROUPS)
        o_turned = signal("o_turned", GROUPS)
        att_out = signal("att_out", GROUPS)
        att_turned = signal("att_turned", TT)
        att_hi = signal("att_hi", TT)
        att_lo = signal("att_lo", TT)
        projected = signal("projected", TT)
        h2_out = signal("h2_out", TT)
        ln2_out = signal("ln2_out", TT)
        ln2_turned = signal("ln2_turned", TT)
        ln2_wide = signal("ln2_wide", 2 * TT)
        ln2_lo = signal("ln2_lo", TT)
        gated = signal("gated", TT)
        logit = signal("logit", 1)
        gexp = signal("gexp", 1)
        gweight = signal("gweight", 1)
        gturned = signal("gturned", 1)
        gt_out = signal("gt_out", 1)
        b2_done = signal("b2_done", 2)
        att_v = Chain(sem("att_v"))
        accn_ready = signal("accn_ready", 2)
        handed_x = signal("handed_x", 1)
        handed_acc = signal("handed_acc", 2)
        z_ready = signal("z_ready", CHUNKS)
        h_hi = signal("h_hi", 2 * CHUNKS)
        h_lo = signal("h_lo", CHUNKS)
        f2_done = signal("f2_done", CHUNKS)
        gate_unscaled = signal("gate_unscaled", EXPERTS)
        acc_done = signal("acc_done", EXPERTS * TT)
        stored = signal("stored", 16)

        block = ctx.enter_context(nc.Block())

        def run(eng, steps):
            for stage, n in first_order:
                steps(stage, n, None, 0)
            for stage, n in second_order:
                steps(stage, n, 0, 1)
            with eng.Fori(1, BATCHES - 1) as i:
                for stage, n in merged:
                    steps(stage, n, i, i + 1)
            for stage, n in last_order:
                steps(stage, n, BATCHES - 1, None)

        @block.sync
        def _(sp):
            for dst, src in ((ident, unit), (gatew, gate_w.rearrange("(k p) e -> p k e", p=P)), (b1raw, b1_t),
                             (cos, rope_cos), (sin, rope_sin), (b2sb, b2),
                             (qkvb, qkv_b.partition_broadcast(P)), (outb, out_b.partition_broadcast(P)),
                             (gateb, gate_b.partition_broadcast(P))):
                sp.dma_start(dst[:], src).then_inc(consts_in, 16)
            taps = raw[:, 0:TAPS * D].rearrange("p (t o) -> p t o", t=TAPS)
            sums = raw[:, TAPS * D:(TAPS + DK) * D].rearrange("p (k o) -> p k o", k=DK)
            sp.dma_start(taps, mix_w.partition_broadcast(P)).then_inc(raw_in, 16)
            sp.dma_start(sums, mix_sum_t.rearrange("(k p) o -> p k o", p=P)).then_inc(raw_in, 16)
            sp.wait_ge(raw_used, 2)
            sp.dma_start(raw[:, 0:DK * QKV].rearrange("p (k n) -> p k n", k=DK),
                         qkv_w_t.rearrange("(k p) n -> p k n", p=P)).then_inc(raw_in, 16)
            sp.dma_start(raw[:, DK * QKV:DK * (QKV + D)].rearrange("p (k n) -> p k n", k=DK),
                         out_w_t.rearrange("(k p) n -> p k n", p=P)).then_inc(raw_in, 16)

            def load_x(b):
                for t in range(TT):
                    wait(sp, x_lo, b, t - 1)
                    wait(sp, x_hi, b, t - 1)
                    sp.dma_start(xraw[t % 2][:], x_t[b * TT + t]).then_inc(x_in[t % 2].sem, 16)

            def load_raw(e):
                sp.wait_ge(raw_used, 4 + 2 * e)
                sp.dma_start(raw[:, 0:2048].rearrange("p (k n) -> p k n", k=DK),
                             w1[e].rearrange("(k p) n -> p k n", p=P)).then_inc(raw_in, 16)
                sp.dma_start(raw[:, 2048:4096].rearrange("p (k n) -> p k n", k=HM),
                             w2[e].rearrange("(k p) n -> p k n", p=P)).then_inc(raw_in, 16)

            def store_parts(e):
                sp.wait_ge(parts_hi, 2 * e + 2)
                sp.wait_ge(parts_lo, 2 * e + 2)
                sp.dma_start(w1_parts[e], w1s[e % 2][:]).then_inc(parts_out[e % 2], 16)
                sp.dma_start(w2_parts[e], w2s[e % 2][:]).then_inc(parts_out[e % 2], 16)

            def load_expert(b, e):
                s = e % 2
                wait(sp, z_ready, b, HM * (e - 1))
                sp.dma_start(w1s[s][:], w1_parts[e]).then_inc(w1_in[s].sem, 16)
                wait(sp, f2_done, b, HM * (e - 1))
                sp.dma_start(w2s[s][:], w2_parts[e]).then_inc(w2_in[s].sem, 16)

            def store(b):
                wait(sp, acc_done, b, EXPERTS * TT)
                sp.dma_start(out[b].rearrange("(t p) d -> p t d", p=P), acc[:]).then_inc(stored.sem, 16)

            load_x(0)
            load_raw(0)
            for e in range(2):
                load_raw(e + 1)
                store_parts(e)
            load_x(1)
            for e in range(2, EXPERTS):
                if e + 1 < EXPERTS:
                    load_raw(e + 1)
                store_parts(e)
            for done in parts_out:
                sp.wait_ge(done, 32 * EXPERTS // 2)
            load_expert(1, 0)
            load_expert(1, 1)
            store(0)

            def body(b, more):
                if more:
                    load_x(b + 1)
                for e in range(2, EXPERTS):
                    load_expert(b, e)
                if more:
                    load_expert(b + 1, 0)
                    load_expert(b + 1, 1)
                store(b)

            with sp.Fori(1, BATCHES - 1) as i:
                body(i, True)
            body(BATCHES - 1, False)
            sp.wait_ge(stored.sem, 16 * BATCHES)

        @block.gpsimd
        def _(pool):
            def steps(stage, n, fb, ab):
                if stage == "f1":
                    wait(pool, h_hi, fb, 2 * (n + 1))
                    wait(pool, f2_done, fb, n - HBUFS + 1)
                    pool.tensor_tensor(hl[n % HBUFS][:], h32[n % 2][:], hh[n % HBUFS][:], ALU.subtract)\
                        .then_inc(h_lo.sem, 1)
                elif stage == "maxima":
                    pool.wait_ge(maxima, 3 * (n + 1))
                    if n:
                        pool.wait_ge(scales, n)
                    pool.partition_all_reduce(mxr[:], mx[:], P, bass.bass_isa.ReduceOp.max).then_inc(maxima_all, 1)
                elif stage == "qkv" and n == TT - 1:
                    wait(pool, ln1_out, ab, TT)
                    pool.tensor_tensor(resid[:], resid[:], outb[:].unsqueeze(1).broadcast_to([P, TT, D]),
                                       ALU.add).then_inc(resid_biased.sem, 1)

            pool.wait_ge(consts_in, 16 * 9)
            run(pool, steps)

        @block.scalar
        def _(act):
            def copy(out_ap, in_ap):
                return act.activation(out_ap, in_ap, ACT.Copy)

            act.wait_ge(set_v.sem, 1 + XK // DK * DK)
            copy(mix[:, 0].rearrange("p k o -> p (k o)"),
                 probs[0][:].rearrange("p j t -> p (j t)")).then_inc(set_hi, 1)
            act.wait_ge(raw_in, 64)
            copy(qkvw[:, 0].rearrange("p k n -> p (k n)"), raw[:, 0:DK * QKV]).then_inc(set_hi, 1)
            copy(outw[:, 0].rearrange("p k n -> p (k n)"),
                 raw[:, DK * QKV:DK * (QKV + D)]).then_inc(set_hi, 1)

            def split_x(b, t):
                wait(act, x_in[t % 2], b, 16 * (t // 2 + 1))
                wait(act, mixed, b, t)
                copy(xh[:], xraw[t % 2][:]).then_inc(x_hi.sem, 1)

            def steps(stage, n, fb, ab):
                if stage == "split":
                    split_x(ab, n)
                elif stage == "ln1_turn":
                    wait(act, ln1_turned, ab, n + 1)
                    wait(act, qkv_done, ab, n)
                    wait(act, projected, ab, 0)
                    copy(turned_h[:], turn_ps[:, 0:DK, :]).then_inc(ln1_hi.sem, 1)
                elif stage == "stack":
                    wait(act, qk_unit, ab, n + 1)
                    wait(act, stack_turned, ab, n)
                    copy(stack[:, :, :, 0, :], tmp_a[:].rearrange("p (a h d) -> p a h d", a=2, d=HD))\
                        .then_inc(stack_hi.sem, 1)
                elif stage == "qk_turn":
                    wait(act, stack_turned, ab, n + 1)
                    wait(act, scored, ab, 0)
                    copy(qt[:, :, n * P:(n + 1) * P],
                         bank_s[0][:, :].bitcast(F16).rearrange("p (h t) -> p h t", t=P)).then_inc(qt_out.sem, 1)
                elif stage == "scores":
                    u, half = divmod(n, 2)
                    if half == 0:
                        wait(act, weighed, ab, u - 1)
                    for j in range(2):
                        wait(act, scored, ab, 2 * n + j + 1)
                        act.activation(probs[u % 2][:, 2 * half + j, :], bank_s[j][:, :], ACT.Exp,
                                       scale=SCORE_SCALE).then_inc(exped.sem, 1)
                elif stage == "out_turn":
                    wait(act, weighed, ab, 4 * (n + 1))
                    wait(act, o_turned, ab, n)
                    copy(osb[:], bank_o[:, :]).then_inc(o_out.sem, 1)
                elif stage == "att_turn":
                    wait(act, att_turned, ab, n + 1)
                    wait(act, projected, ab, n)
                    wait(act, qkv_done, ab, TT)
                    copy(turned_h[:], turn_ps[:, 0:DK, :]).then_inc(att_hi.sem, 1)
                elif stage == "ln2_turn":
                    wait(act, ln2_turned, ab, n + 1)
                    wait(act, gated, ab, n)
                    wait(act, ln2_lo, ab, n)
                    copy(wide[:], turn_ps[:, 0:DK, :]).then_inc(ln2_wide.sem, 1)
                    wait(act, handed_x, ab, 0)
                    copy(x16n[:, 0, :, n * P:(n + 1) * P], turn_ps[:, 0:DK, :]).then_inc(ln2_wide.sem, 1)
                elif stage == "gates":
                    wait(act, logit, ab, 1)
                    act.activation(eg[:], lg[:], ACT.Exp, scale=-1.0).then_inc(gexp.sem, 1)
                elif stage == "gates_turn":
                    wait(act, gturned, ab, 1)
                    copy(wt[:, :], bank_m[0:EXPERTS, :]).then_inc(gt_out.sem, 1)
                elif stage == "f1":
                    e, m = divmod(n, HM)
                    wait(act, z_ready, fb, n + 1)
                    wait(act, h_lo, fb, n - 1)
                    act.activation(h32[n % 2][:], bank_h[n % 2][:, :], ACT.Relu,
                                   bias=b1s[:, e, m:m + 1]).then_inc(h_hi.sem, 1)
                    wait(act, f2_done, fb, n - HBUFS + 1)
                    act.activation(hh[n % HBUFS][:], bank_h[n % 2][:, :], ACT.Relu,
                                   bias=b1s[:, e, m:m + 1]).then_inc(h_hi.sem, 1)
                elif stage == "parts1":
                    s = n % 2
                    act.wait_ge(scales, n + 1)
                    if n >= 2:
                        act.wait_ge(parts_out[s], 32 * (n // 2))
                        wait(act, z_ready, 0, HM * (n - 1))
                    act.activation(w1s[s][:, 0].rearrange("p k n -> p (k n)"), raw[:, 0:2048], ACT.Copy,
                                   scale=scl[:, 0:1]).then_inc(parts_hi, 1)
                elif stage == "parts2":
                    if n >= 2:
                        wait(act, f2_done, 0, HM * (n - 1))
                    act.activation(w2s[n % 2][:, 0].rearrange("p k n -> p (k n)"), raw[:, 2048:4096], ACT.Copy,
                                   scale=scl[:, 1:2]).then_inc(parts_hi, 1)

            run(act, steps)

        @block.tensor
        def _(pe):
            def parts(out_ap, high, low, w, lo_w, start=True, stop=True):
                n = len(high)
                for k in range(n):
                    pe.matmul(out_ap, high[k], w[k], start=start and k == 0, stop=False, skip_group_check=True)
                    pe.matmul(out_ap, high[k], lo_w[k], start=False, stop=False, skip_group_check=True)
                    last = pe.matmul(out_ap, low[k], w[k], start=False, stop=stop and k == n - 1,
                                     skip_group_check=True)
                return last

            def turn(signal_, source):
                for k in range(DK):
                    last = pe.transpose(turn_ps[:, k, :], source(k), ident[:])
                last.then_inc(signal_.sem, 1)

            def steps(stage, n, fb, ab):
                if stage == "mix":
                    wait(pe, x_hi, ab, n + 1)
                    wait(pe, x_lo, ab, n + 1)
                    wait(pe, mixed_out, ab, 2 * (n - 1))
                    if n < 2:
                        wait(pe, accn_ready, ab, 0)
                    last = parts(bank_s[n % 2][:, 0:D], [xh[:, k, :] for k in range(XK)],
                                 [xl[:, k, :] for k in range(XK)], [mix[:, 0, k, :] for k in range(XK)],
                                 [mix[:, 1, k, :] for k in range(XK)])
                    last.then_inc(mixed.sem, 1)
                elif stage == "ln1_turn":
                    wait(pe, ln1_out, ab, n + 1)
                    wait(pe, ln1_lo, ab, n)
                    if n == 0:
                        wait(pe, gt_out, ab, 0)
                    turn(ln1_turned, lambda k: normed[:, n, k * P:(k + 1) * P])
                elif stage == "qkv":
                    wait(pe, ln1_hi, ab, n + 1)
                    wait(pe, ln1_lo, ab, n + 1)
                    wait(pe, mixed_out, ab, 2 * TT)
                    wait(pe, qkv_out, ab, 2 * n)
                    high = [turned_h[:, k, :] for k in range(DK)]
                    low = [turned_l[:, k, :] for k in range(DK)]
                    parts(bank_s[0][:, :], high, low, [qkvw[:, 0, k, 0:2 * D] for k in range(DK)],
                          [qkvw[:, 1, k, 0:2 * D] for k in range(DK)])
                    last = parts(bank_s[1][:, 0:D], high, low, [qkvw[:, 0, k, 2 * D:QKV] for k in range(DK)],
                                 [qkvw[:, 1, k, 2 * D:QKV] for k in range(DK)])
                    last.then_inc(qkv_done.sem, 1)
                elif stage == "qk_turn":
                    wait(pe, stack_ready, ab, 2 * (n + 1))
                    wait(pe, qkv_out, ab, 2 * TT)
                    wait(pe, qt_out, ab, n)
                    wait(pe, kt_out, ab, n)
                    for a in range(2):
                        turned = bank_s[a][:, :].bitcast(F16).rearrange("p (h t) -> p h t", t=P)
                        for h in range(HEADS // 2):
                            last = pe.transpose(turned[:, h, :],
                                                stack[:, a, 2 * h:2 * h + 2, :, :].rearrange("p h s d -> p (h s d)"),
                                                ident16[:])
                    last.then_inc(stack_turned.sem, 1)
                elif stage == "scores":
                    (g, tile), half = divmod(n // 2, TT), n % 2
                    if n == 0:
                        wait(pe, qt_out, ab, TT)
                        wait(pe, kt_out, ab, TT)
                    for j in range(2):
                        h = 4 * g + 2 * half + j
                        lo = 64 * j
                        wait(pe, exped, ab, 2 * n + j - 1)
                        pe.matmul(bank_s[j][:, :], kt[lo:lo + 64, h // 2, tile * P:(tile + 1) * P],
                                  qt[lo:lo + 64, h // 2, :], start=True, stop=True).then_inc(scored.sem, 1)
                elif stage == "weigh":
                    g, tile = divmod(n, TT)
                    wait(pe, exped, ab, 4 * (n + 1))
                    if n == 0:
                        wait(pe, qkv_out, ab, 2 * TT)
                        wait(pe, logit, ab, 0)
                    if tile == 0:
                        wait(pe, o_out, ab, g)
                    for j in range(4):
                        h = 4 * g + j
                        last = pe.matmul(bank_o[32 * j:32 * j + 32, :],
                                         v1[:, tile, h, :, :].rearrange("p s d -> p (s d)"),
                                         probs[n % 2][:, j, :], start=(tile == 0), stop=(tile == TT - 1),
                                         skip_group_check=True)
                    last.then_inc(weighed.sem, 1)
                elif stage == "out_turn":
                    wait(pe, o_out, ab, n + 1)
                    wait(pe, att_out, ab, n)
                    wait(pe, ln1_lo, ab, TT)
                    for t in range(TT):
                        last = pe.transpose(turn_ps[:, t, :], osb[:, t * P:(t + 1) * P], ident[:])
                    last.then_inc(o_turned.sem, 1)
                elif stage == "att_turn":
                    wait(pe, att_out, ab, GROUPS)
                    wait(pe, att_lo, ab, n)
                    turn(att_turned, lambda k: att[:, n, k * P:(k + 1) * P])
                elif stage == "project":
                    wait(pe, att_hi, ab, n + 1)
                    wait(pe, att_lo, ab, n + 1)
                    wait(pe, exped, ab, 4 * UNITS)
                    wait(pe, h2_out, ab, n - 1)
                    last = parts(bank_s[n % 2][:, 0:D], [turned_h[:, k, :] for k in range(DK)],
                                 [turned_l[:, k, :] for k in range(DK)], [outw[:, 0, k, :] for k in range(DK)],
                                 [outw[:, 1, k, :] for k in range(DK)])
                    last.then_inc(projected.sem, 1)
                elif stage == "ln2_turn":
                    wait(pe, ln2_out, ab, n + 1)
                    wait(pe, att_lo, ab, TT)
                    wait(pe, ln2_wide, ab, 2 * n)
                    turn(ln2_turned, lambda k: normed[:, n, k * P:(k + 1) * P])
                elif stage == "logits":
                    wait(pe, ln2_wide, ab, 2 * n + 1)
                    if n == 0:
                        wait(pe, o_out, ab, GROUPS)
                    for k in range(DK):
                        last = pe.matmul(bank_o[:, n * EXPERTS:(n + 1) * EXPERTS], wide[:, k, :], gatew[:, k, :],
                                         start=(k == 0), stop=(k == DK - 1), skip_group_check=True)
                    last.then_inc(gated.sem, 1)
                elif stage == "gates_turn":
                    wait(pe, gweight, ab, 1)
                    wait(pe, ln2_wide, ab, 2 * TT)
                    for t in range(TT):
                        last = pe.transpose(bank_m[0:EXPERTS, t * P:(t + 1) * P], wg[:, t, :], ident[:])
                    last.then_inc(gturned.sem, 1)
                elif stage == "bias2":
                    wait(pe, gt_out, ab, 1)
                    wait(pe, h2_out, ab, TT)
                    for t in range(TT):
                        last = pe.matmul(bank_s[t // 2][:, t % 2 * D:(t % 2 + 1) * D], wt[:, t * P:(t + 1) * P],
                                         b2sb[:, :], start=True, stop=True, skip_group_check=True)
                        if t % 2:
                            last.then_inc(b2_done.sem, 1)
                elif stage == "f1":
                    e, m = divmod(n, HM)
                    if n == 0:
                        wait(pe, handed_x, fb, 1)
                    if m == 0 and isinstance(fb, int) and fb == 0:
                        pe.wait_ge(parts_lo, 2 * e + 1)
                    elif m == 0:
                        wait(pe, w1_in[e % 2], fb - 1, 16 * (e // 2 + 1))
                    wait(pe, h_hi, fb, 2 * (n - 1))
                    w = w1s[e % 2]
                    for k in range(DK):
                        for wp, xp in ((0, 0), (0, 1), (1, 0)):
                            last = pe.matmul(bank_h[n % 2][:, :], w[:, wp, k, m * P:(m + 1) * P], x16[:, xp, k, :],
                                             start=(k == 0 and wp + xp == 0), stop=(k == DK - 1 and wp == 1),
                                             skip_group_check=True)
                    last.then_inc(z_ready.sem, 1)
                elif stage == "f2":
                    e, m = divmod(n, HM)
                    wait(pe, h_lo, fb, n + 1)
                    if m == 0 and isinstance(fb, int) and fb == 0:
                        pe.wait_ge(parts_lo, 2 * e + 2)
                    elif m == 0:
                        wait(pe, w2_in[e % 2], fb - 1, 16 * (e // 2 + 1))
                    w = w2s[e % 2]
                    for t in range(TT):
                        if m == 0 and t % 2 == 0:
                            wait(pe, acc_done, fb, TT * (e - 1) + t + 2)
                        o = bank_f[t // 2][:, t % 2 * D:(t % 2 + 1) * D]
                        high, low = hh[n % HBUFS][:, t * P:(t + 1) * P], hl[n % HBUFS][:, t * P:(t + 1) * P]
                        pe.matmul(o, high, w[:, 0, m, :], start=(m == 0 and t % 2 == 0), stop=False,
                                  skip_group_check=True)
                        pe.matmul(o, high, w[:, 1, m, :], start=False, stop=False, skip_group_check=True)
                        last = pe.matmul(o, low, w[:, 0, m, :], start=False, stop=(m == HM - 1),
                                         skip_group_check=True)
                    last.then_inc(f2_done.sem, 1)

            pe.wait_ge(consts_in, 16 * 9)
            pe.wait_ge(weights_ready, 1)
            run(pe, steps)

        @block.vector
        def _(dve):
            dve.wait_ge(consts_in, 16 * 9)
            dve.memset(v1[:, :, :, 1, :], 1.0)
            set_v.link(dve, dve.tensor_copy(ident16[:], ident[:]))
            dve.wait_ge(raw_in, 32)
            taps = raw[:, 0:TAPS * D].rearrange("p (t o) -> p t o", t=TAPS)
            sums = raw[:, TAPS * D:(TAPS + DK) * D].rearrange("p (k o) -> p k o", k=DK)
            made = probs[0][:].rearrange("p j t -> p (j t)").rearrange("p (k o) -> p k o", o=D)
            for t in range(TAPS):
                for k in range(DK):
                    ins = dve.tensor_tensor(made[:, t * DK + k, :], sums[:, k, :], taps[:, t, :], ALU.mult)
                    set_v.link(dve, ins)
            dve.wait_ge(set_hi, 1)
            dve.tensor_tensor(mix[:, 1].rearrange("p k o -> p (k o)"), probs[0][:].rearrange("p j t -> p (j t)"),
                              mix[:, 0].rearrange("p k o -> p (k o)").bitcast(F32), ALU.subtract)\
                .then_inc(raw_used, 2)
            dve.wait_ge(raw_in, 64)
            dve.wait_ge(set_hi, 3)
            dve.tensor_tensor(qkvw[:, 1].rearrange("p k n -> p (k n)"), raw[:, 0:DK * QKV],
                              qkvw[:, 0].rearrange("p k n -> p (k n)").bitcast(F32), ALU.subtract)\
                .then_inc(raw_used, 1)
            set_v.link(dve, dve.tensor_tensor(outw[:, 1].rearrange("p k n -> p (k n)"),
                                              raw[:, DK * QKV:DK * (QKV + D)],
                                              outw[:, 0].rearrange("p k n -> p (k n)").bitcast(F32),
                                              ALU.subtract))
            dve.memset(ones[:], 1.0).then_inc(raw_used, 1)
            dve.wait_ge(raw_used, 4)
            dve.tensor_scalar(ones[:], ones[:], 1.0, None, ALU.mult).then_inc(weights_ready, 1)

            def rsqrt(v, n):
                a, b, c = y1[:, 0:n], y2[:, 0:n], y3[:, 0:n]
                att_v.link(dve, dve.tensor_scalar(b.bitcast(I32), v.bitcast(I32), 1, None,
                                                  ALU.logical_shift_right))
                att_v.link(dve, dve.tensor_scalar(a.bitcast(I32), b.bitcast(I32), -1.0, float(RSQRT_GUESS),
                                                  ALU.mult, ALU.add))
                for _ in range(4):
                    att_v.link(dve, dve.scalar_tensor_tensor(b, a, -0.5, a, ALU.mult, ALU.mult))
                    att_v.link(dve, dve.tensor_tensor(c, b, v, ALU.mult))
                    att_v.link(dve, dve.scalar_tensor_tensor(a, c, 1.5, a, ALU.add, ALU.mult))

            def norm_scale(b):
                dve.tensor_tensor(gap[:], stats[:, :, 0, 1], stats[:, :, 1, 1], ALU.subtract)
                dve.tensor_tensor(mean[:], stats[:, :, 0, 1], stats[:, :, 1, 1], ALU.add)
                att_v.link(dve, dve.tensor_tensor(var[:], stats[:, :, 0, 2], stats[:, :, 1, 2], ALU.add))
                dve.tensor_scalar(mean[:], mean[:], 0.5, None, ALU.mult)
                att_v.link(dve, dve.scalar_tensor_tensor(gap[:], gap[:], 0.25, gap[:], ALU.mult, ALU.mult))
                att_v.link(dve, dve.scalar_tensor_tensor(var[:], var[:], 1.0 / D, gap[:], ALU.mult, ALU.add))
                att_v.link(dve, dve.tensor_scalar(var[:], var[:], LN_EPS, None, ALU.add))
                rsqrt(var[:], TT)

            def steps(stage, n, fb, ab):
                if stage == "split":
                    if n == 0:
                        att_v.start(ab)
                    wait(dve, x_hi, ab, n + 1)
                    wait(dve, mixed, ab, n)
                    wait(dve, x_in[n % 2], ab, 16 * (n // 2 + 1))
                    dve.tensor_tensor(xl[:], xraw[n % 2][:], xh[:].bitcast(F32), ALU.subtract)\
                       .then_inc(x_lo.sem, 1)
                elif stage == "mix":
                    wait(dve, mixed, ab, n + 1)
                    dve.tensor_copy(resid[:, n, :], bank_s[n % 2][:, 0:D]).then_inc(mixed_out.sem, 1)
                    dve.bn_stats(stats[:, n].rearrange("p h s -> p (h s)"), bank_s[n % 2][:, 0:D])\
                       .then_inc(mixed_out.sem, 1)
                elif stage == "ln1":
                    wait(dve, mixed_out, ab, 2 * TT)
                    norm_scale(ab)
                    wait(dve, ln2_turned, ab, 0)
                    for t in range(TT):
                        dve.tensor_scalar(normed[:, t, :], resid[:, t, :], mean[:, t:t + 1], y1[:, t:t + 1],
                                          ALU.subtract, ALU.mult).then_inc(ln1_out.sem, 1)
                elif stage == "ln1_turn":
                    wait(dve, ln1_hi, ab, n + 1)
                    wait(dve, qkv_done, ab, n)
                    dve.tensor_tensor(turned_l[:], turn_ps[:, 0:DK, :], turned_h[:].bitcast(F32), ALU.subtract)\
                       .then_inc(ln1_lo.sem, 1)
                elif stage == "qkv":
                    wait(dve, qkv_done, ab, n + 1)
                    if n == 0:
                        wait(dve, weighed, ab, 0)
                    att_v.link(dve, dve.tensor_tensor(qk[:, n, :], bank_s[0][:, :], qkvb[:, 0:2 * D], ALU.add))
                    dve.tensor_tensor(v1[:, n, :, 0, :], bank_s[1][:, 0:D].rearrange("p (h d) -> p h d", d=HD),
                                      qkvb[:, 2 * D:QKV].rearrange("p (h d) -> p h d", d=HD), ALU.add)\
                       .then_inc(qkv_out.sem, 2)
                elif stage == "rotate":
                    row = qk[:, n, :]
                    att_v.link(dve, dve.tensor_tensor(tmp_a[:], row, row, ALU.mult))
                    att_v.link(dve, dve.tensor_reduce(ss[:, n, :], tmp_a[:].rearrange("p (h d) -> p h d", d=HD),
                                                      AX.X, ALU.add))
                    heads = row.rearrange("p (h d) -> p h d", d=HD)
                    c = cos[:, n, :].unsqueeze(1).broadcast_to([P, 2 * HEADS, HD])
                    dve.tensor_tensor(tmp_a[:].rearrange("p (h d) -> p h d", d=HD), heads, c, ALU.mult)
                    pairs = row.rearrange("p (h f two) -> p h f two", f=HD // 2, two=2)
                    swapped = tmp_b[:].rearrange("p (h f two) -> p h f two", f=HD // 2, two=2)
                    sines = sin[:, n, :].rearrange("p (f two) -> p f two", two=2)
                    for side in range(2):
                        s = sines[:, :, side].unsqueeze(1).broadcast_to([P, 2 * HEADS, HD // 2])
                        ins = dve.tensor_tensor(swapped[:, :, :, side], pairs[:, :, :, 1 - side], s, ALU.mult)
                    att_v.link(dve, ins)
                    att_v.link(dve, dve.tensor_tensor(row, tmp_a[:], tmp_b[:], ALU.add))
                elif stage == "qk_norm":
                    flat = ss[:].rearrange("p t h -> p (t h)")
                    att_v.link(dve, dve.tensor_scalar(flat, flat, NORM_EPS * NORM_EPS, None, ALU.max))
                    rsqrt(flat, TT * 2 * HEADS)
                elif stage == "stack":
                    wait(dve, stack_hi, ab, n)
                    scale = y1[:, n * 2 * HEADS:(n + 1) * 2 * HEADS].unsqueeze(2)\
                        .broadcast_to([P, 2 * HEADS, HD])
                    dve.tensor_tensor(tmp_a[:].rearrange("p (h d) -> p h d", d=HD),
                                      qk[:, n, :].rearrange("p (h d) -> p h d", d=HD), scale, ALU.mult)\
                       .then_inc(qk_unit.sem, 1)
                    wait(dve, stack_hi, ab, n + 1)
                    wait(dve, stack_turned, ab, n)
                    both = tmp_a[:].rearrange("p (a h d) -> p a h d", a=2, d=HD)
                    wait(dve, qk_unit, ab, n + 1)
                    dve.tensor_tensor(stack[:, 0, :, 1, :], both[:, 0], stack[:, 0, :, 0, :], ALU.subtract)
                    att_v.link(dve, dve.tensor_tensor(stack[:, 1, :, 2, :], both[:, 1], stack[:, 1, :, 0, :],
                                                      ALU.subtract))
                    dve.tensor_copy(stack[:, 0, :, 2:4, :], stack[:, 0, :, 0:2, :]).then_inc(stack_ready.sem, 1)
                    for s in (0, 2):
                        ins = dve.tensor_copy(stack[:, 1, :, s + 1, :], stack[:, 1, :, s, :])
                    ins.then_inc(stack_ready.sem, 1)
                elif stage == "qk_turn":
                    wait(dve, stack_turned, ab, n + 1)
                    wait(dve, scored, ab, 0)
                    dve.tensor_copy(kt[:, :, n * P:(n + 1) * P],
                                    bank_s[1][:, :].bitcast(F16).rearrange("p (h t) -> p h t", t=P))\
                       .then_inc(kt_out.sem, 1)
                elif stage == "out_turn":
                    wait(dve, o_turned, ab, n + 1)
                    rows = bank_m[:, :].rearrange("p (t j d) -> p t j d", t=TT, j=4)
                    att_v.link(dve, dve.reciprocal(rc[:], rows[:, :, :, HD]))
                    if n == 0:
                        wait(dve, att_turned, ab, 0)
                    dve.tensor_tensor(att[:, :, n * 4 * HD:(n + 1) * 4 * HD].rearrange("p t (j d) -> p t j d", d=HD),
                                      rows[:, :, :, 0:HD], rc[:].unsqueeze(3).broadcast_to([P, TT, 4, HD]),
                                      ALU.mult).then_inc(att_out.sem, 1)
                elif stage == "att_turn":
                    wait(dve, att_hi, ab, n + 1)
                    wait(dve, projected, ab, n)
                    dve.tensor_tensor(turned_l[:], turn_ps[:, 0:DK, :], turned_h[:].bitcast(F32), ALU.subtract)\
                       .then_inc(att_lo.sem, 1)
                elif stage == "project":
                    wait(dve, projected, ab, n + 1)
                    wait(dve, resid_biased, ab, 1)
                    wait(dve, handed_acc, ab, 0)
                    ins = dve.tensor_tensor(accn[:, n, :], bank_s[n % 2][:, 0:D], resid[:, n, :], ALU.add)
                    ins.then_inc(h2_out.sem, 1)
                    wait(dve, h2_out, ab, n + 1)
                    att_v.link(dve, dve.bn_stats(stats[:, n].rearrange("p h s -> p (h s)"), accn[:, n, :]))
                elif stage == "ln2":
                    norm_scale(ab)
                    wait(dve, ln1_turned, ab, TT)
                    for t in range(TT):
                        dve.tensor_scalar(normed[:, t, :], accn[:, t, :], mean[:, t:t + 1], y1[:, t:t + 1],
                                          ALU.subtract, ALU.mult).then_inc(ln2_out.sem, 1)
                elif stage == "ln2_turn":
                    wait(dve, ln2_wide, ab, 2 * (n + 1))
                    cut = slice(n * P, (n + 1) * P)
                    dve.tensor_tensor(x16n[:, 1, :, cut], wide[:], x16n[:, 0, :, cut], ALU.subtract)\
                       .then_inc(ln2_lo.sem, 1)
                elif stage == "gates":
                    wait(dve, gated, ab, TT)
                    dve.tensor_tensor(lg[:], bank_o[:, 0:TT * EXPERTS].rearrange("p (t e) -> p t e", t=TT),
                                      gateb[:].unsqueeze(1).broadcast_to([P, TT, EXPERTS]), ALU.add)\
                       .then_inc(logit.sem, 1)
                    wait(dve, gexp, ab, 1)
                    att_v.link(dve, dve.tensor_scalar(pg[:], eg[:], 1.0, None, ALU.add))
                    att_v.link(dve, dve.reciprocal(pg[:], pg[:]))
                    wait(dve, gturned, ab, 0)
                    flat = [z[:].rearrange("p t e -> p (t e)") for z in (wg, lg, pg)]
                    dve.scalar_tensor_tensor(flat[0], flat[1], 0.0, flat[2], ALU.is_gt, ALU.mult)\
                       .then_inc(gweight.sem, 1)
                    wait(dve, gweight, ab, 1)
                    dve.tensor_copy(gwn[:], wg[:]).then_inc(accn_ready.sem, 1)
                elif stage == "bias2":
                    wait(dve, b2_done, ab, 2)
                    for s in range(2):
                        cut = accn[:, 2 * s:2 * s + 2, :].rearrange("p t d -> p (t d)")
                        ins = dve.tensor_tensor(cut, bank_s[s][:, :], cut, ALU.add)
                    ins.then_inc(accn_ready.sem, 1)
                elif stage == "hand_x":
                    if fb is not None:
                        wait(dve, z_ready, fb, CHUNKS)
                    wait(dve, ln2_lo, ab, TT)
                    dve.tensor_copy(x16[:], x16n[:]).then_inc(handed_x.sem, 1)
                elif stage == "hand_acc":
                    if fb is not None:
                        wait(dve, stored, fb, 16)
                        wait(dve, acc_done, fb, EXPERTS * TT)
                    wait(dve, accn_ready, ab, 2)
                    dve.tensor_copy(gw[:], gwn[:]).then_inc(handed_acc.sem, 1)
                    dve.tensor_copy(acc[:], accn[:]).then_inc(handed_acc.sem, 1)
                elif stage == "acc":
                    wait(dve, f2_done, fb, HM * (n + 1))
                    wait(dve, handed_acc, fb, 2)
                    wait(dve, acc_done, fb, TT * n)
                    dve.tensor_scalar(gs[:], gw[:, :, n], unscale[:, n:n + 1], None, ALU.mult)\
                       .then_inc(gate_unscaled.sem, 1)
                    wait(dve, gate_unscaled, fb, n + 1)
                    for t in range(TT):
                        dve.scalar_tensor_tensor(acc[:, t, :], bank_f[t // 2][:, t % 2 * D:(t % 2 + 1) * D],
                                                 gs[:, t:t + 1], acc[:, t, :], ALU.mult, ALU.add)\
                           .then_inc(acc_done.sem, 1)
                elif stage == "maxima":
                    maxima_and_scales(n)
                elif stage in ("parts1", "parts2"):
                    low_parts(n, stage == "parts2")

            def maxima_and_scales(e):
                dve.wait_ge(raw_in, 64 + 32 * (e + 1))
                if e:
                    dve.wait_ge(maxima_all, e)
                dve.tensor_reduce(mx[:, 0:1], raw[:, 0:2048], AX.X, ALU.max, apply_absolute_value=True)\
                   .then_inc(maxima, 1)
                dve.tensor_reduce(mx[:, 1:2], raw[:, 2048:4096], AX.X, ALU.max, apply_absolute_value=True)\
                   .then_inc(maxima, 1)
                dve.tensor_reduce(mx[:, 2:3], b1raw[:, e, :], AX.X, ALU.max, apply_absolute_value=True)\
                   .then_inc(maxima, 1)
                dve.wait_ge(maxima_all, e + 1)
                set_v.link(dve, dve.scalar_tensor_tensor(bound[:, 0:1], mxr[:, 0:1], float(D), mxr[:, 2:3],
                                                         ALU.mult, ALU.add))
                set_v.link(dve, dve.tensor_copy(bound[:, 1:2], mxr[:, 1:2]))
                set_v.link(dve, dve.tensor_scalar(bound[:], bound[:], FLOOR, None, ALU.max))
                set_v.link(dve, dve.tensor_scalar(pow2[:].bitcast(I32), bound[:].bitcast(I32), EXPONENT, None,
                                                  ALU.bitwise_and))
                set_v.link(dve, dve.tensor_scalar(inv2[:].bitcast(I32), pow2[:].bitcast(I32), -1.0,
                                                  float(2 * ONE_BITS), ALU.mult, ALU.add))
                if e:
                    dve.wait_ge(parts_hi, 2 * e)
                set_v.link(dve, dve.tensor_scalar(scl[:], inv2[:], TOP, None, ALU.mult))
                set_v.link(dve, dve.scalar_tensor_tensor(unscale[:, e:e + 1], pow2[:, 0:1], TOP ** -2, pow2[:, 1:2],
                                                         ALU.mult, ALU.mult))
                dve.tensor_scalar(b1s[:, e, :], b1raw[:, e, :], scl[:, 0:1], None, ALU.mult).then_inc(scales, 1)

            def low_parts(e, second):
                w, cut = (w2s[e % 2], raw[:, 2048:4096]) if second else (w1s[e % 2], raw[:, 0:2048])
                dve.wait_ge(parts_hi, 2 * e + second + 1)
                dve.scalar_tensor_tensor(w[:, 1].rearrange("p k n -> p (k n)"), cut, scl[:, second:second + 1],
                                         w[:, 0].rearrange("p k n -> p (k n)"), ALU.mult, ALU.subtract)\
                   .then_inc(parts_lo, 1)
                if second:
                    dve.wait_ge(parts_lo, 2 * e + 2)
                    dve.tensor_scalar(ones[:], ones[:], 1.0, None, ALU.mult).then_inc(raw_used, 2)

            run(dve, steps)


_OUTS = [((8, 512, 256), "float32")]


def _rope_tables(np):
    pos = np.arange(TOKENS, dtype=np.float32)
    half = HD // 2
    inv = (np.float32(1.0) / np.power(np.float32(2500), np.arange(half, dtype=np.float32) / np.float32(half)))
    theta = (pos[:, None] * inv.astype(np.float32)[None, :]).astype(np.float32)
    s, c = np.sin(theta), np.cos(theta)
    cos = np.repeat(c, 2, axis=1)
    sin = np.stack([-s, s], axis=-1).reshape(TOKENS, HD)
    return [np.ascontiguousarray(a.reshape(TT, P, HD).transpose(1, 0, 2)).astype(np.float32) for a in (cos, sin)]


def kernel(**inputs):
    import numpy as _np
    import concourse.bacc as _bacc
    from concourse import mybir as _mybir
    from concourse.bass_utils import run_bass_kernel_spmd as _run

    i = {k: _np.asarray(v) for k, v in inputs.items()}
    x_t = i["x"].reshape(BATCHES * TT, P, DK, P, TAPS).transpose(0, 3, 4, 2, 1).reshape(BATCHES * TT, P, XK, P)
    cos, sin = _rope_tables(_np)
    laid = {
        "x_t": x_t,
        "mix_w": i["L0_tok_weight"].T,
        "mix_sum_t": i["L0_tok_weighted_sum"].T,
        "qkv_w_t": i["L0_attn_qkv_w"].T,
        "qkv_b": i["L0_attn_qkv_b"],
        "out_w_t": i["L0_attn_out_w"].T,
        "out_b": i["L0_attn_out_b"],
        "gate_w": i["L0_ffn_Wg"],
        "gate_b": i["L0_ffn_bg"],
        "w1": i["L0_ffn_W1"],
        "b1_t": i["L0_ffn_b1"].reshape(EXPERTS, HM, P).transpose(2, 0, 1),
        "w2": i["L0_ffn_W2"],
        "b2": i["L0_ffn_b2"],
        "rope_cos": cos,
        "rope_sin": sin,
        "unit": _np.eye(P, dtype=_np.float32),
    }
    nc = _bacc.Bacc("TRN2", target_bir_lowering=False, num_devices=1)
    arrays, args = {}, []
    for name, a in laid.items():
        a = _np.ascontiguousarray(a)
        arrays[f"in_{name}_dram"] = a
        args.append(nc.dram_tensor(f"in_{name}_dram", a.shape, _mybir.dt.from_np(a.dtype), kind="ExternalInput").ap())
    for n, (shape, dtype) in enumerate(_OUTS):
        dt = _mybir.dt.from_np(_np.dtype(dtype))
        args.append(nc.dram_tensor(f"out_{n}_dram", shape, dt, kind="ExternalOutput").ap())
    build(nc, *args)
    r = _run(nc, [arrays], core_ids=[0])
    got = tuple(r.results[0][f"out_{n}_dram"] for n in range(len(_OUTS)))
    return got[0]
```

```python
from contextlib import ExitStack

import concourse.bass as bass
from concourse import mybir

F32 = mybir.dt.float32
F32R = mybir.dt.float32r
F16 = mybir.dt.float16
I32 = mybir.dt.int32
ALU = mybir.AluOpType
ACT = mybir.ActivationFunctionType
AX = mybir.AxisListType

P = 128
BATCHES = 8
TOKENS = 512
TT = TOKENS // P
D = 256
DK = D // P
TAPS = 4
XK = D * TAPS // P
HEADS = 16
HD = D // HEADS
GROUPS = HEADS // 4
QKV = 3 * D
EXPERTS = 8
HIDDEN = 1024
HM = HIDDEN // P
CHUNKS = EXPERTS * HM
LAG = 3
HBUFS = 4
UNITS = GROUPS * TT
LN_EPS = 1e-5
NORM_EPS = 1e-12
SCORE_SCALE = HD ** -0.5
ONE_BITS = 127 << 23
EXPONENT = 0x7F800000
RSQRT_GUESS = 0x5F3759DF
TOP = 2.0 ** 14
FLOOR = 2.0 ** -40


def attention_order(alone=False):
    steps = []
    for t in range(TT):
        steps += [(MIX[t - 1] - 0.05 if t else 0.3, "split", t), (MIX[t], "mix", t),
                  (9.0 + 1.5 * t, "ln1_turn", t), (10.55 + 1.5 * t, "qkv", t), (10.6 + 1.5 * t, "rotate", t),
                  (17.1 + 1.5 * t, "unit", t), (18.6 + 1.5 * t, "stack", t), (20 + 1.5 * t, "qk_turn", t)]
    steps += [(6.8, "ln1", 0), (13.65, "qk_norm", 0), (15.8, "qk_norm", 1)]
    if alone:
        order = ["ln1_turn 0", "ln1_turn 1", "qkv 0", "rotate 0", "ln1_turn 2", "qkv 1", "rotate 1", "qk_norm 0",
                 "unit 0", "ln1_turn 3", "qkv 2", "stack 0", "rotate 2", "unit 1", "qkv 3", "qk_turn 0", "stack 1",
                 "rotate 3", "qk_norm 1", "qk_turn 1", "unit 2", "stack 2", "unit 3", "qk_turn 2", "stack 3",
                 "qk_turn 3"]
        places = {name: 8 + 0.1 * k for k, name in enumerate(order)}
        steps = [(places.get(f"{stage} {n}", at), stage, n) for at, stage, n in steps]
    first = 25.6
    for n in range(2 * UNITS):
        steps.append((first + PACE * n, "scores", n))
    for u in range(UNITS):
        steps.append((first + PACE * (2 * u + 3) + 0.1, "weigh", u))
    for g in range(GROUPS):
        steps += [(first + PACE * (8 * (g + 1) + 1) + 0.15, "out_copy", g),
                  (first + PACE * (8 * (g + 1) + 3) + 0.2, "out_turn", g)]
    tail = first + PACE * (2 * UNITS + 4) + 1
    for t in range(TT):
        steps += [(tail + t, "att_turn", t), (tail + t + 1.1, "project", t), (tail + 7.6 + 0.8 * t, "ln2_turn", t),
                  (tail + 8.5 + 0.8 * t, "logits", t)]
    steps += [(tail + 5.2, "ln2", 0), (tail + 11.2, "gates", 0), (tail + 12.7, "gates_turn", 0),
              (tail + 13.7, "bias2", 0)]
    steps.sort(key=lambda s: s[0])
    return steps


PACE = 0.66
MIX = [2.1, 3.5, 4.9, 6.3]
PIECES = 4


def bodies():
    attention = attention_order()
    prep = [(0.4 + 0.9 * p, "parts", PIECES + p) for p in range(PIECES)]
    for e in range(2, EXPERTS):
        start = HM * (e - 1)
        early = (-4.0, -2.3, -1.6, -1.3, 2.3, 3.1, 3.9, 4.7)
        late = (1.7, 2.6, 3.6, 3.9, 4.6, 5.3, 6.0, 6.8)
        stages = [("maxima", 2 * e), ("maxima", 2 * e + 1), ("reduce", e), ("scales", e)]
        stages += [("parts", PIECES * e + p) for p in range(PIECES)]
        prep += [(start + at, *stage) for at, stage in zip(early if e == 2 else late, stages)]

    def merge(waiting, hand, done=0):
        waiting, order = sorted(waiting, key=lambda s: s[0]), []
        for c in range(CHUNKS + LAG):
            if c < CHUNKS:
                if c >= done:
                    order.append(("f1", c))
                if c == HM // 2:
                    order.append(("hand_acc", 0))
                while waiting and waiting[0][0] < c + 0.5:
                    order.append(waiting.pop(0)[1:])
            else:
                while waiting:
                    order.append(waiting.pop(0)[1:])
                if hand and c == CHUNKS:
                    order.append(("hand_x", 0))
            if c >= LAG:
                order.append(("f2", c - LAG))
                if (c - LAG) % HM == HM - 1:
                    order.append(("acc", (c - LAG) // HM))
            while waiting and waiting[0][0] < c + 1:
                order.append(waiting.pop(0)[1:])
        return order

    between = {("split", 0): [("mix_weights", 1)], ("split", 1): [("projections", 0)],
               ("scores", 3): [("maxima", 0), ("maxima", 1), ("reduce", 0), ("scales", 0)],
               ("scores", 7): [("parts", 0)], ("scores", 11): [("parts", 1)],
               ("scores", 15): [("parts", 2)], ("scores", 19): [("parts", 3)],
               ("scores", 31): [("maxima", 2), ("maxima", 3), ("reduce", 1), ("scales", 1)],
               ("logits", TT - 1): [("hand_x", 0), ("f1", 0)],
               ("gates", 0): [("f1", 1)]}
    first = [("mix_weights", 0)]
    for step in attention_order(alone=True):
        first += [step[1:]] + between.get(step[1:], [])
    return first, merge(attention + prep, True, done=2), merge(attention, True), merge([], False)


def exps_first(order):
    order = list(order)
    for k in range(len(order) - 1):
        if order[k][0] == "f1" and order[k + 1][0] == "scores":
            order[k], order[k + 1] = order[k + 1], order[k]
    return order


class Signal:

    def __init__(self, sem, per_batch):
        self.sem, self.per_batch = sem, per_batch

    def at(self, batch, count):
        return batch * self.per_batch + count


def wait(eng, signal, batch, count):
    value = signal.at(batch, count)
    if not (isinstance(value, int) and value <= 0):
        eng.wait_ge(signal.sem, value)


class Chain:

    def __init__(self, sem):
        self.sem, self.per_batch, self.count = sem, None, 0

    def start(self, batch):
        if self.count:
            self.per_batch = self.count
        self.batch, self.count = batch, 0

    def link(self, eng, ins):
        ins.then_inc(self.sem, 1)
        self.count += 1
        base = 0 if self.per_batch is None else self.batch * self.per_batch
        eng.wait_ge(self.sem, base + self.count)


def build(nc, x_t, mix_w, mix_sum_t, qkv_w_t, qkv_b, out_w_t, out_b, gate_w, gate_b, w1, b1_t, w2, b2,
          rope_cos, rope_sin, unit, out):
    first_order, second_order, merged, last_order = bodies()
    w1_parts = nc.dram_tensor("w1_parts", [EXPERTS, P, 2, DK, HIDDEN], F16, kind="Internal").ap()
    w2_parts = nc.dram_tensor("w2_parts", [EXPERTS, P, 2, HM, D], F16, kind="Internal").ap()

    with ExitStack() as ctx:
        def sb(name, shape, dt=F32):
            return ctx.enter_context(nc.sbuf_tensor(name, shape, dt))

        def bank(name):
            return ctx.enter_context(nc.psum_tensor(name, [P, 512], F32))

        def sem(name):
            return ctx.enter_context(nc.semaphore(name))

        def signal(name, per_batch):
            return Signal(sem(name), per_batch)

        ident = sb("ident", [P, P])
        ident16 = sb("ident16", [P, P], F16)
        mix = sb("mix", [P, 2, XK, D], F32R)
        qkvw = sb("qkvw", [P, 2, DK, QKV], F32R)
        outw = sb("outw", [P, 2, DK, D], F32R)
        qkvb = sb("qkvb", [P, QKV])
        outb = sb("outb", [P, D])
        gatew = sb("gatew", [P, DK, EXPERTS])
        gateb = sb("gateb", [P, EXPERTS])
        b2sb = sb("b2sb", [EXPERTS, D])
        b1raw = sb("b1raw", [P, EXPERTS, HM])
        b1s = sb("b1s", [P, EXPERTS, HM])
        cos = sb("cos", [P, TT, HD])
        sin = sb("sin", [P, TT, HD])
        unscale = sb("unscale", [P, EXPERTS])

        raw = sb("raw", [P, 4096])
        w1s = [sb(f"w1s{i}", [P, 2, DK, HIDDEN], F16) for i in range(2)]
        w2s = [sb(f"w2s{i}", [P, 2, HM, D], F16) for i in range(2)]
        xraw = [sb(f"xraw{i}", [P, XK, P]) for i in range(2)]

        resid = sb("resid", [P, TT, D])
        normed = sb("normed", [P, TT, D])
        turned_h = sb("turned_h", [P, 2, DK, P], F32R)
        turned_l = sb("turned_l", [P, 2, DK, P], F32R)
        qk = sb("qk", [P, TT, 2 * D])
        tmp_a = sb("tmp_a", [P, 2 * D])
        tmp_b = sb("tmp_b", [P, 2 * D])
        stack = sb("stack", [P, 2, HEADS, 4, HD], F16)
        qt = sb("qt", [P, HEADS // 2, TOKENS], F16)
        kt = sb("kt", [P, HEADS // 2, TOKENS], F16)
        v1 = sb("v1", [P, TT, HEADS, 2, HD])
        probs = [sb(f"probs{i}", [P, 4, TOKENS]) for i in range(2)]
        xh = sb("xh", [P, XK, P], F32R)
        xl = sb("xl", [P, XK, P], F32R)
        units_at = probs[1]
        squares = probs[0][:, 0, :]
        osb = tmp_b
        att = normed
        stats = sb("stats", [P, TT, 2, 3])
        mean = sb("mean", [P, TT])
        var = sb("var", [P, TT])
        gap = sb("gap", [P, TT])
        ss = sb("ss", [P, TT, 2 * HEADS])
        y1 = sb("y1", [P, TT * 2 * HEADS])
        y2 = sb("y2", [P, TT * 2 * HEADS])
        y3 = sb("y3", [P, TT * 2 * HEADS])
        rc = sb("rc", [P, TT, 4])
        wide = sb("wide", [P, 2, DK, P])
        lg = sb("lg", [P, TT, EXPERTS])
        eg = sb("eg", [P, TT, EXPERTS])
        pg = sb("pg", [P, TT, EXPERTS])
        wg = sb("wg", [P, TT, EXPERTS])
        wt = tmp_a[0:EXPERTS, :]
        x16n = sb("x16n", [P, 2, DK, TOKENS], F16)
        x16 = sb("x16", [P, 2, DK, TOKENS], F16)
        gwn = sb("gwn", [P, TT, EXPERTS])
        gw = sb("gw", [P, TT, EXPERTS])
        gs = sb("gs", [P, TT])
        accn = sb("accn", [P, TT, D])
        acc = sb("acc", [P, TT, D])
        h32 = [sb(f"h32_{i}", [P, TOKENS]) for i in range(2)]
        hh = [sb(f"hh{i}", [P, TOKENS], F16) for i in range(HBUFS)]
        hl = [sb(f"hl{i}", [P, TOKENS], F16) for i in range(HBUFS)]
        mx = sb("mx", [P, 3])
        mxr = sb("mxr", [P, 3])
        bound = sb("bound", [P, 2])
        pow2 = sb("pow2", [P, 2])
        inv2 = sb("inv2", [P, 2])
        scl = sb("scl", [P, 2])

        bank_s = [bank(f"bank_s{i}") for i in range(2)]
        bank_m = bank("bank_m")
        bank_o = bank("bank_o")
        bank_h = [bank(f"bank_h{i}") for i in range(2)]
        bank_f = [bank(f"bank_f{i}") for i in range(2)]
        turn_ps = bank_m[:, :].rearrange("p (k t) -> p k t", t=P)
        tile_ps = [b[:, 0:DK * P].rearrange("p (k t) -> p k t", t=P) for b in (bank_m, bank_o)]

        consts_in = sem("consts_in")
        pool_consts = sem("pool_consts")
        mix_in = [sem(f"mix_in{i}") for i in range(2)]
        proj_in = sem("proj_in")
        mix_made = [sem(f"mix_made{i}") for i in range(2)]
        set_hi = sem("set_hi")
        set_lo = sem("set_lo")
        raw_in = [sem(f"raw_in{i}") for i in range(2)]
        maxima = sem("maxima")
        maxima_all = sem("maxima_all")
        scales = sem("scales")
        scale_v = Chain(sem("scale_v"))
        parts_hi = sem("parts_hi")
        parts_lo = sem("parts_lo")
        parts_out = [sem(f"parts_out{i}") for i in range(2)]
        w1_in = [signal(f"w1_in{i}", 16 * EXPERTS // 2) for i in range(2)]
        w2_in = [signal(f"w2_in{i}", 16 * EXPERTS // 2) for i in range(2)]
        x_in = [signal(f"x_in{i}", 16 * TT // 2) for i in range(2)]
        x_hi = signal("x_hi", 2 * TT)
        x_lo = signal("x_lo", 2 * TT)
        x_used = signal("x_used", 2 * TT)
        mixed_out = signal("mixed_out", 2 * TT)
        ln1_out = signal("ln1_out", TT)
        ln1_turned = signal("ln1_turned", TT)
        ln1_hi = signal("ln1_hi", TT)
        ln1_lo = signal("ln1_lo", TT)
        resid_biased = signal("resid_biased", 1)
        qkv_done = signal("qkv_done", TT)
        qkv_out = signal("qkv_out", 2 * TT)
        squared = signal("squared", TT)
        cosined = signal("cosined", TT)
        summed = signal("summed", TT)
        qk_unit = signal("qk_unit", TT)
        stack_hi = signal("stack_hi", 2 * TT)
        stack_ready = signal("stack_ready", 2 * TT)
        stack_turned = signal("stack_turned", 2 * TT)
        qt_out = signal("qt_out", TT)
        kt_out = signal("kt_out", TT)
        scored = signal("scored", 4 * UNITS)
        exped = signal("exped", 4 * UNITS)
        weighed = signal("weighed", UNITS)
        o_out = signal("o_out", GROUPS)
        o_turned = signal("o_turned", GROUPS)
        att_out = signal("att_out", GROUPS)
        att_turned = signal("att_turned", TT)
        att_hi = signal("att_hi", TT)
        att_lo = signal("att_lo", TT)
        projected = signal("projected", TT)
        h2_out = signal("h2_out", TT)
        ln2_out = signal("ln2_out", TT)
        ln2_turned = signal("ln2_turned", TT)
        ln2_wide = signal("ln2_wide", 2 * TT)
        ln2_lo = signal("ln2_lo", TT)
        gated = signal("gated", TT)
        logit = signal("logit", 1)
        gexp = signal("gexp", 1)
        gweight = signal("gweight", 1)
        gturned = signal("gturned", 1)
        gt_out = signal("gt_out", 1)
        b2_done = signal("b2_done", 2)
        att_v = Chain(sem("att_v"))
        accn_ready = signal("accn_ready", 2)
        handed_x = signal("handed_x", 1)
        handed_acc = signal("handed_acc", 2)
        z_ready = signal("z_ready", CHUNKS)
        h_hi = signal("h_hi", 2 * CHUNKS)
        h_lo = signal("h_lo", CHUNKS)
        f2_done = signal("f2_done", CHUNKS)
        gate_unscaled = signal("gate_unscaled", EXPERTS)
        acc_done = signal("acc_done", EXPERTS * TT)
        stored = signal("stored", 32)

        block = ctx.enter_context(nc.Block())

        def score_bank(n, alone):
            return ([bank_s[0], bank_s[1], bank_h[0], bank_h[1]] if alone else bank_s)[n % (4 if alone else 2)]

        def qkv_banks(t, alone):
            return bank_h if alone and t % 2 else bank_s

        def qk_turn_bank(a, alone):
            return (bank_f if alone else bank_s)[a][:, :].bitcast(F16).rearrange("p (h t) -> p h t", t=P)

        def stack_slots(t, a):
            high, low = ((stack[:, 0, :, 0:4:2, :], stack[:, 0, :, 1:4:2, :]) if a == 0 else
                         (stack[:, 1, :, 0:2, :], stack[:, 1, :, 2:4, :]))
            values = units_at[:, t % 2, a * D:(a + 1) * D].rearrange("p (h d) -> p h d", d=HD)
            return high, low, values.unsqueeze(2).broadcast_to([P, HEADS, 2, HD])

        def piece(p, part):
            half, quarter = divmod(p % PIECES, PIECES // 2)
            w = (w2s if half else w1s)[p // PIECES % 2]
            cut = slice(1024 * quarter, 1024 * (quarter + 1))
            return (w[:, part].rearrange("p k n -> p (k n)")[:, cut],
                    raw[:, 2048 * half:2048 * (half + 1)][:, cut], scl[:, half:half + 1])

        def run(eng, steps):
            def ordered(steps_):
                return exps_first(steps_) if eng is nc.scalar else steps_
            for stage, n in first_order:
                steps(stage, n, 0 if stage == "f1" else None, 0)
            for stage, n in ordered(second_order):
                steps(stage, n, 0, 1)
            with eng.Fori(1, BATCHES - 1) as i:
                for stage, n in ordered(merged):
                    steps(stage, n, i, i + 1)
            for stage, n in last_order:
                steps(stage, n, BATCHES - 1, None)

        taps = raw[:, 0:TAPS * D].rearrange("p (t o) -> p t o", t=TAPS)
        sums = raw[:, TAPS * D:(TAPS + DK) * D].rearrange("p (k o) -> p k o", k=DK)
        raw_qkv = raw[:, 2048:2048 + DK * QKV]
        raw_out = raw[:, 2048 + DK * QKV:2048 + DK * (QKV + D)]
        made = probs[0][:].rearrange("p j t -> p (j t)")
        half_x = [slice(XK // 2 * i, XK // 2 * (i + 1)) for i in range(2)]
        half_mix = [slice(XK // 2 * D * i, XK // 2 * D * (i + 1)) for i in range(2)]
        flat_mix = [mix[:, part].rearrange("p k o -> p (k o)") for part in range(2)]

        def make_mix(eng, half):
            rows = made.rearrange("p (k o) -> p k o", o=D)
            eng.wait_ge(mix_in[0], 32)
            if half:
                eng.wait_ge(mix_in[1], 16)
            for k in range(XK)[half_x[half]]:
                ins = eng.tensor_tensor(rows[:, k, :], sums[:, k % DK, :], taps[:, k // DK, :], ALU.mult)
            ins.then_inc(mix_made[half], 1)

        @block.sync
        def _(sp):
            def load_x(b, tiles):
                for t in tiles:
                    wait(sp, x_lo, b, 2 * (t - 1))
                    wait(sp, x_hi, b, 2 * (t - 1))
                    sp.dma_start(xraw[t % 2][:], x_t[b * TT + t]).then_inc(x_in[t % 2].sem, 16)

            sp.dma_start(sums, mix_sum_t.rearrange("(k p) o -> p k o", p=P)).then_inc(mix_in[0], 16)
            sp.dma_start(taps[:, 0:TAPS // 2], mix_w[0:TAPS // 2].partition_broadcast(P)).then_inc(mix_in[0], 16)
            sp.dma_start(taps[:, TAPS // 2:TAPS], mix_w[TAPS // 2:TAPS].partition_broadcast(P))\
              .then_inc(mix_in[1], 16)
            load_x(0, [0])
            sp.dma_start(raw_qkv.rearrange("p (k n) -> p k n", k=DK),
                         qkv_w_t.rearrange("(k p) n -> p k n", p=P)).then_inc(proj_in, 16)
            sp.dma_start(raw_out.rearrange("p (k n) -> p k n", k=DK),
                         out_w_t.rearrange("(k p) n -> p k n", p=P)).then_inc(proj_in, 16)
            load_x(0, [1])
            for dst, src in ((ident, unit), (qkvb, qkv_b.partition_broadcast(P)), (cos, rope_cos), (sin, rope_sin),
                             (outb, out_b.partition_broadcast(P)), (gatew, gate_w.rearrange("(k p) e -> p k e", p=P)),
                             (gateb, gate_b.partition_broadcast(P)), (b1raw, b1_t), (b2sb, b2)):
                sp.dma_start(dst[:], src).then_inc(consts_in, 16)
            load_x(0, [2, 3])

            def load_raw(e):
                if e:
                    sp.wait_ge(parts_lo, PIECES * (e - 1) + PIECES // 2)
                else:
                    sp.wait_ge(set_lo, 4)
                sp.dma_start(raw[:, 0:2048].rearrange("p (k n) -> p k n", k=DK),
                             w1[e].rearrange("(k p) n -> p k n", p=P)).then_inc(raw_in[0], 16)
                if e:
                    sp.wait_ge(parts_lo, PIECES * e)
                sp.dma_start(raw[:, 2048:4096].rearrange("p (k n) -> p k n", k=HM),
                             w2[e].rearrange("(k p) n -> p k n", p=P)).then_inc(raw_in[1], 16)

            def store_parts(e):
                sp.wait_ge(parts_hi, PIECES * (e + 1))
                sp.wait_ge(parts_lo, PIECES * (e + 1))
                sp.dma_start(w1_parts[e], w1s[e % 2][:]).then_inc(parts_out[e % 2], 16)
                sp.dma_start(w2_parts[e], w2s[e % 2][:]).then_inc(parts_out[e % 2], 16)

            def load_expert(b, e):
                s = e % 2
                wait(sp, z_ready, b, HM * (e - 1))
                sp.dma_start(w1s[s][:], w1_parts[e]).then_inc(w1_in[s].sem, 16)
                wait(sp, f2_done, b, HM * (e - 1))
                sp.dma_start(w2s[s][:], w2_parts[e]).then_inc(w2_in[s].sem, 16)

            def store(b):
                for half in range(2):
                    tiles = slice(TT // 2 * half, TT // 2 * (half + 1))
                    wait(sp, acc_done, b, EXPERTS * TT - TT // 2 * (1 - half))
                    sp.dma_start(out[b].rearrange("(t p) d -> p t d", p=P)[:, tiles], acc[:, tiles])\
                      .then_inc(stored.sem, 16)

            load_raw(0)
            load_x(1, [0, 1])
            load_raw(1)
            store_parts(0)
            load_x(1, [2, 3])
            load_raw(2)
            store_parts(1)
            for e in range(2, EXPERTS):
                if e + 1 < EXPERTS:
                    load_raw(e + 1)
                store_parts(e)
            for done in parts_out:
                sp.wait_ge(done, 32 * EXPERTS // 2)
            load_x(2, [0, 1])
            load_expert(1, 0)
            load_expert(1, 1)
            store(0)

            def body(b, more, far):
                if more:
                    load_x(b + 1, [2, 3])
                for e in range(2, EXPERTS):
                    load_expert(b, e)
                if far:
                    load_x(b + 2, [0, 1])
                if more:
                    load_expert(b + 1, 0)
                    load_expert(b + 1, 1)
                store(b)

            with sp.Fori(1, BATCHES - 2) as i:
                body(i, True, True)
            body(BATCHES - 2, True, False)
            body(BATCHES - 1, False, False)
            sp.wait_ge(stored.sem, 32 * BATCHES)

        @block.gpsimd
        def _(pool):
            def steps(stage, n, fb, ab):
                if stage == "f1":
                    wait(pool, h_hi, fb, 2 * (n + 1))
                    wait(pool, f2_done, fb, n - HBUFS + 1)
                    pool.tensor_tensor(hl[n % HBUFS][:], h32[n % 2][:], hh[n % HBUFS][:], ALU.subtract)\
                        .then_inc(h_lo.sem, 1)
                elif stage == "rotate":
                    wait(pool, qkv_out, ab, 2 * n + 1)
                    wait(pool, summed, ab, n)
                    wait(pool, b2_done, ab, 0)
                    pool.tensor_tensor(tmp_a[:].rearrange("p (h d) -> p h d", d=HD),
                                       qk[:, n, :].rearrange("p (h d) -> p h d", d=HD),
                                       cos[:, n, :].unsqueeze(1).broadcast_to([P, 2 * HEADS, HD]), ALU.mult)\
                        .then_inc(cosined.sem, 1)
                elif stage == "reduce":
                    pool.wait_ge(maxima, 3 * (n + 1))
                    if n:
                        pool.wait_ge(scales, n)
                    pool.partition_all_reduce(mxr[:], mx[:], P, bass.bass_isa.ReduceOp.max).then_inc(maxima_all, 1)
                elif stage == "qkv" and n == TT - 1:
                    wait(pool, ln1_out, ab, TT)
                    pool.tensor_tensor(resid[:], resid[:], outb[:].unsqueeze(1).broadcast_to([P, TT, D]),
                                       ALU.add).then_inc(resid_biased.sem, 1)

            make_mix(pool, 1)
            pool.memset(v1[:, :, :, 1, :], 1.0).then_inc(pool_consts, 1)
            pool.wait_ge(consts_in, 16 * 9)
            pool.tensor_copy(ident16[:], ident[:]).then_inc(pool_consts, 1)
            run(pool, steps)

        @block.scalar
        def _(act):
            def copy(out_ap, in_ap):
                return act.activation(out_ap, in_ap, ACT.Copy)

            def take_turned(t, a, b, alone):
                dst, done = ((qt, qt_out), (kt, kt_out))[a]
                wait(act, stack_turned, b, 2 * t + a + 1)
                wait(act, scored, b, 0)
                copy(dst[:, :, t * P:(t + 1) * P], qk_turn_bank(a, alone)).then_inc(done.sem, 1)

            def split_x(b, t):
                wait(act, x_in[t % 2], b, 16 * (t // 2 + 1))
                for half in range(2):
                    wait(act, x_used, b, 2 * (t - 1) + half + 1)
                    copy(xh[:, half_x[half]], xraw[t % 2][:, half_x[half]]).then_inc(x_hi.sem, 1)

            def steps(stage, n, fb, ab):
                if stage == "split":
                    split_x(ab, n)
                elif stage == "mix_weights":
                    act.wait_ge(mix_made[n], 1)
                    copy(flat_mix[0][:, half_mix[n]], made[:, half_mix[n]]).then_inc(set_hi, 1)
                elif stage == "projections":
                    act.wait_ge(proj_in, 32)
                    copy(qkvw[:, 0].rearrange("p k n -> p (k n)"), raw_qkv).then_inc(set_hi, 1)
                    copy(outw[:, 0].rearrange("p k n -> p (k n)"), raw_out).then_inc(set_hi, 1)
                elif stage == "ln1_turn":
                    wait(act, ln1_turned, ab, n + 1)
                    if n >= 2:
                        wait(act, qkv_done, ab, n - 1)
                    wait(act, projected, ab, 0)
                    copy(turned_h[:, n % 2], tile_ps[n % 2]).then_inc(ln1_hi.sem, 1)
                elif stage == "rotate":
                    wait(act, qkv_out, ab, 2 * n + 1)
                    wait(act, summed, ab, n)
                    wait(act, weighed, ab, 0)
                    act.activation(squares, qk[:, n, :], ACT.Square).then_inc(squared.sem, 1)
                elif stage == "stack":
                    wait(act, qk_unit, ab, n + 1)
                    for a in range(2):
                        wait(act, stack_turned, ab, 2 * (n - 1) + a + 1)
                        high, _, unit_qk = stack_slots(n, a)
                        copy(high, unit_qk).then_inc(stack_hi.sem, 1)
                        if n:
                            take_turned(n - 1, a, ab, fb is None)
                elif stage == "qk_turn" and n == TT - 1:
                    for a in range(2):
                        take_turned(n, a, ab, fb is None)
                elif stage == "scores":
                    u, half = divmod(n, 2)
                    if half == 0:
                        wait(act, weighed, ab, u - 1)
                    for j in range(2):
                        wait(act, scored, ab, 2 * n + j + 1)
                        act.activation(probs[u % 2][:, 2 * half + j, :], score_bank(2 * n + j, fb is None)[:, :], ACT.Exp,
                                       scale=SCORE_SCALE).then_inc(exped.sem, 1)
                elif stage == "out_copy":
                    wait(act, weighed, ab, 4 * (n + 1))
                    wait(act, o_turned, ab, n)
                    copy(osb[:], bank_o[:, :]).then_inc(o_out.sem, 1)
                elif stage == "att_turn":
                    wait(act, att_turned, ab, n + 1)
                    if n >= 2:
                        wait(act, projected, ab, n - 1)
                    wait(act, qkv_done, ab, TT)
                    copy(turned_h[:, n % 2], tile_ps[n % 2]).then_inc(att_hi.sem, 1)
                elif stage == "ln2_turn":
                    wait(act, ln2_turned, ab, n + 1)
                    if n >= 2:
                        wait(act, gated, ab, n - 1)
                        wait(act, ln2_lo, ab, n - 1)
                    copy(wide[:, n % 2], tile_ps[n % 2]).then_inc(ln2_wide.sem, 1)
                    wait(act, handed_x, ab, 0)
                    copy(x16n[:, 0, :, n * P:(n + 1) * P], tile_ps[n % 2]).then_inc(ln2_wide.sem, 1)
                elif stage == "gates":
                    wait(act, logit, ab, 1)
                    act.activation(eg[:], lg[:], ACT.Exp, scale=-1.0).then_inc(gexp.sem, 1)
                elif stage == "gates_turn":
                    wait(act, gturned, ab, 1)
                    copy(wt, bank_m[0:EXPERTS, :]).then_inc(gt_out.sem, 1)
                elif stage == "f1":
                    e, m = divmod(n, HM)
                    wait(act, z_ready, fb, n + 1)
                    wait(act, h_lo, fb, n - 1)
                    act.activation(h32[n % 2][:], bank_h[n % 2][:, :], ACT.Relu,
                                   bias=b1s[:, e, m:m + 1]).then_inc(h_hi.sem, 1)
                    wait(act, f2_done, fb, n - HBUFS + 1)
                    act.activation(hh[n % HBUFS][:], bank_h[n % 2][:, :], ACT.Relu,
                                   bias=b1s[:, e, m:m + 1]).then_inc(h_hi.sem, 1)
                elif stage == "parts" and n >= PIECES:
                    e, p = divmod(n, PIECES)
                    act.wait_ge(scales, e + 1)
                    if e >= 2 and p == 0:
                        act.wait_ge(parts_out[e % 2], 32 * (e // 2))
                        wait(act, z_ready, 0, HM * (e - 1))
                    if e >= 2 and p == PIECES // 2:
                        wait(act, f2_done, 0, HM * (e - 1))
                    high, cut, scale = piece(n, 0)
                    act.activation(high, cut, ACT.Copy, scale=scale).then_inc(parts_hi, 1)

            run(act, steps)

        @block.tensor
        def _(pe):
            def parts(out_ap, high, low, w, lo_w, start=True, stop=True):
                n = len(high)
                for k in range(n):
                    pe.matmul(out_ap, high[k], w[k], start=start and k == 0, stop=False, skip_group_check=True)
                    pe.matmul(out_ap, high[k], lo_w[k], start=False, stop=False, skip_group_check=True)
                    last = pe.matmul(out_ap, low[k], w[k], start=False, stop=stop and k == n - 1,
                                     skip_group_check=True)
                return last

            def turn(signal_, t, source):
                for k in range(DK):
                    last = pe.transpose(tile_ps[t % 2][:, k, :], source(k), ident[:])
                last.then_inc(signal_.sem, 1)

            def steps(stage, n, fb, ab):
                if stage == "mix":
                    wait(pe, mixed_out, ab, 2 * (n - 1))
                    if n < 2:
                        wait(pe, accn_ready, ab, 0)
                    for half in range(2):
                        if n == 0 and fb is None:
                            pe.wait_ge(set_lo, half + 1)
                        wait(pe, x_hi, ab, 2 * n + half + 1)
                        wait(pe, x_lo, ab, 2 * n + half + 1)
                        ks = range(XK)[half_x[half]]
                        last = parts(bank_s[n % 2][:, 0:D], [xh[:, k, :] for k in ks], [xl[:, k, :] for k in ks],
                                     [mix[:, 0, k, :] for k in ks], [mix[:, 1, k, :] for k in ks],
                                     start=half == 0, stop=half == 1)
                        last.then_inc(x_used.sem, 1)
                elif stage == "ln1_turn":
                    wait(pe, ln1_out, ab, n + 1)
                    if n >= 2:
                        wait(pe, ln1_lo, ab, n - 1)
                    elif n == 1:
                        wait(pe, ln2_wide, ab, 0)
                    else:
                        wait(pe, gt_out, ab, 0)
                    if n == 0 and fb is None:
                        pe.wait_ge(consts_in, 16 * 9)
                    turn(ln1_turned, n, lambda k: normed[:, n, k * P:(k + 1) * P])
                elif stage == "qkv":
                    wait(pe, ln1_hi, ab, n + 1)
                    wait(pe, ln1_lo, ab, n + 1)
                    wait(pe, mixed_out, ab, 2 * TT)
                    if fb is None and n >= 2:
                        wait(pe, qkv_out, ab, 2 * (n - 1))
                    elif fb is not None:
                        wait(pe, qkv_out, ab, 2 * n)
                    at_qk, at_v = qkv_banks(n, fb is None)
                    if n == 0 and fb is None:
                        pe.wait_ge(set_lo, 4)
                    high = [turned_h[:, n % 2, k, :] for k in range(DK)]
                    low = [turned_l[:, n % 2, k, :] for k in range(DK)]
                    parts(at_qk[:, :], high, low, [qkvw[:, 0, k, 0:2 * D] for k in range(DK)],
                          [qkvw[:, 1, k, 0:2 * D] for k in range(DK)])
                    last = parts(at_v[:, 0:D], high, low, [qkvw[:, 0, k, 2 * D:QKV] for k in range(DK)],
                                 [qkvw[:, 1, k, 2 * D:QKV] for k in range(DK)])
                    last.then_inc(qkv_done.sem, 1)
                elif stage == "qk_turn":
                    if fb is not None:
                        wait(pe, qkv_out, ab, 2 * TT)
                    if n == 0 and fb is None:
                        pe.wait_ge(pool_consts, 2)
                    for a in range(2):
                        wait(pe, stack_ready, ab, 2 * n + a + 1)
                        wait(pe, (qt_out, kt_out)[a], ab, n)
                        turned = qk_turn_bank(a, fb is None)
                        for h in range(HEADS // 2):
                            last = pe.transpose(turned[:, h, :],
                                                stack[:, a, 2 * h:2 * h + 2, :, :].rearrange("p h s d -> p (h s d)"),
                                                ident16[:])
                        last.then_inc(stack_turned.sem, 1)
                elif stage == "scores":
                    (g, tile), half = divmod(n // 2, TT), n % 2
                    if n == 0:
                        wait(pe, qt_out, ab, TT)
                        wait(pe, kt_out, ab, TT)
                        wait(pe, qkv_out, ab, 2 * TT)
                    for j in range(2):
                        h = 4 * g + 2 * half + j
                        lo = 64 * j
                        wait(pe, exped, ab, 2 * n + j - (3 if fb is None else 1))
                        pe.matmul(score_bank(2 * n + j, fb is None)[:, :], kt[lo:lo + 64, h // 2, tile * P:(tile + 1) * P],
                                  qt[lo:lo + 64, h // 2, :], start=True, stop=True).then_inc(scored.sem, 1)
                elif stage == "weigh":
                    g, tile = divmod(n, TT)
                    wait(pe, exped, ab, 4 * (n + 1))
                    if n == 0:
                        wait(pe, qkv_out, ab, 2 * TT)
                        wait(pe, ln1_lo, ab, TT)
                    if tile == 0:
                        wait(pe, o_out, ab, g)
                    for j in range(4):
                        h = 4 * g + j
                        last = pe.matmul(bank_o[32 * j:32 * j + 32, :],
                                         v1[:, tile, h, :, :].rearrange("p s d -> p (s d)"),
                                         probs[n % 2][:, j, :], start=(tile == 0), stop=(tile == TT - 1),
                                         skip_group_check=True)
                    last.then_inc(weighed.sem, 1)
                elif stage == "out_turn":
                    wait(pe, o_out, ab, n + 1)
                    wait(pe, att_out, ab, n)
                    wait(pe, ln1_lo, ab, TT)
                    for t in range(TT):
                        last = pe.transpose(turn_ps[:, t, :], osb[:, t * P:(t + 1) * P], ident[:])
                    last.then_inc(o_turned.sem, 1)
                elif stage == "att_turn":
                    wait(pe, att_out, ab, GROUPS)
                    if n >= 2:
                        wait(pe, att_lo, ab, n - 1)
                    elif n == 1:
                        wait(pe, o_out, ab, GROUPS)
                    turn(att_turned, n, lambda k: att[:, n, k * P:(k + 1) * P])
                elif stage == "project":
                    wait(pe, att_hi, ab, n + 1)
                    wait(pe, att_lo, ab, n + 1)
                    wait(pe, exped, ab, 4 * UNITS)
                    wait(pe, h2_out, ab, n - 1)
                    last = parts(bank_s[n % 2][:, 0:D], [turned_h[:, n % 2, k, :] for k in range(DK)],
                                 [turned_l[:, n % 2, k, :] for k in range(DK)], [outw[:, 0, k, :] for k in range(DK)],
                                 [outw[:, 1, k, :] for k in range(DK)])
                    last.then_inc(projected.sem, 1)
                elif stage == "ln2_turn":
                    wait(pe, ln2_out, ab, n + 1)
                    wait(pe, att_lo, ab, TT)
                    if n >= 2:
                        wait(pe, ln2_wide, ab, 2 * (n - 1))
                    turn(ln2_turned, n, lambda k: normed[:, n, k * P:(k + 1) * P])
                elif stage == "logits":
                    wait(pe, ln2_wide, ab, 2 * n + 1)
                    if n == 0:
                        wait(pe, h2_out, ab, TT)
                    for k in range(DK):
                        last = pe.matmul(bank_s[0][:, n * EXPERTS:(n + 1) * EXPERTS], wide[:, n % 2, k, :], gatew[:, k, :],
                                         start=(k == 0), stop=(k == DK - 1), skip_group_check=True)
                    last.then_inc(gated.sem, 1)
                elif stage == "gates_turn":
                    wait(pe, gweight, ab, 1)
                    wait(pe, ln2_wide, ab, 2 * TT)
                    for t in range(TT):
                        last = pe.transpose(bank_m[0:EXPERTS, t * P:(t + 1) * P], wg[:, t, :], ident[:])
                    last.then_inc(gturned.sem, 1)
                elif stage == "bias2":
                    wait(pe, gt_out, ab, 1)
                    wait(pe, h2_out, ab, TT)
                    for t in range(TT):
                        last = pe.matmul(bank_s[t // 2][:, t % 2 * D:(t % 2 + 1) * D], wt[:, t * P:(t + 1) * P],
                                         b2sb[:, :], start=True, stop=True, skip_group_check=True)
                        if t % 2:
                            last.then_inc(b2_done.sem, 1)
                elif stage == "f1":
                    e, m = divmod(n, HM)
                    if n == 0:
                        wait(pe, handed_x, fb, 1)
                    if m == 0 and isinstance(fb, int) and fb == 0:
                        pe.wait_ge(parts_lo, PIECES * e + PIECES // 2)
                    elif m == 0:
                        wait(pe, w1_in[e % 2], fb - 1, 16 * (e // 2 + 1))
                    wait(pe, h_hi, fb, 2 * (n - 1))
                    w = w1s[e % 2]
                    for k in range(DK):
                        for wp, xp in ((0, 0), (0, 1), (1, 0)):
                            last = pe.matmul(bank_h[n % 2][:, :], w[:, wp, k, m * P:(m + 1) * P], x16[:, xp, k, :],
                                             start=(k == 0 and wp + xp == 0), stop=(k == DK - 1 and wp == 1),
                                             skip_group_check=True)
                    last.then_inc(z_ready.sem, 1)
                elif stage == "f2":
                    e, m = divmod(n, HM)
                    wait(pe, h_lo, fb, n + 1)
                    if m == 0 and isinstance(fb, int) and fb == 0:
                        pe.wait_ge(parts_lo, PIECES * (e + 1))
                    elif m == 0:
                        wait(pe, w2_in[e % 2], fb - 1, 16 * (e // 2 + 1))
                    w = w2s[e % 2]
                    for t in range(TT):
                        if m == 0 and t % 2 == 0:
                            wait(pe, acc_done, fb, TT * (e - 1) + t + 2)
                        o = bank_f[t // 2][:, t % 2 * D:(t % 2 + 1) * D]
                        high, low = hh[n % HBUFS][:, t * P:(t + 1) * P], hl[n % HBUFS][:, t * P:(t + 1) * P]
                        pe.matmul(o, high, w[:, 0, m, :], start=(m == 0 and t % 2 == 0), stop=False,
                                  skip_group_check=True)
                        pe.matmul(o, high, w[:, 1, m, :], start=False, stop=False, skip_group_check=True)
                        last = pe.matmul(o, low, w[:, 0, m, :], start=False, stop=(m == HM - 1),
                                         skip_group_check=True)
                    last.then_inc(f2_done.sem, 1)

            run(pe, steps)

        @block.vector
        def _(dve):
            def rsqrt(v, cut):
                a, b, c = y1[:, cut], y2[:, cut], y3[:, cut]
                att_v.link(dve, dve.tensor_scalar(b.bitcast(I32), v.bitcast(I32), 1, None,
                                                  ALU.logical_shift_right))
                att_v.link(dve, dve.tensor_scalar(a.bitcast(I32), b.bitcast(I32), -1.0, float(RSQRT_GUESS),
                                                  ALU.mult, ALU.add))
                for _ in range(3):
                    att_v.link(dve, dve.scalar_tensor_tensor(b, a, -0.5, a, ALU.mult, ALU.mult))
                    att_v.link(dve, dve.tensor_tensor(c, b, v, ALU.mult))
                    att_v.link(dve, dve.scalar_tensor_tensor(a, c, 1.5, a, ALU.add, ALU.mult))

            def norm_scale(b):
                dve.tensor_tensor(gap[:], stats[:, :, 0, 1], stats[:, :, 1, 1], ALU.subtract)
                dve.tensor_tensor(mean[:], stats[:, :, 0, 1], stats[:, :, 1, 1], ALU.add)
                att_v.link(dve, dve.tensor_tensor(var[:], stats[:, :, 0, 2], stats[:, :, 1, 2], ALU.add))
                dve.tensor_scalar(mean[:], mean[:], 0.5, None, ALU.mult)
                att_v.link(dve, dve.scalar_tensor_tensor(gap[:], gap[:], 0.25, gap[:], ALU.mult, ALU.mult))
                att_v.link(dve, dve.scalar_tensor_tensor(var[:], var[:], 1.0 / D, gap[:], ALU.mult, ALU.add))
                att_v.link(dve, dve.tensor_scalar(var[:], var[:], LN_EPS, None, ALU.add))
                rsqrt(var[:], slice(0, TT))

            def steps(stage, n, fb, ab):
                if stage == "split":
                    if n == 0:
                        att_v.start(ab)
                    wait(dve, x_in[n % 2], ab, 16 * (n // 2 + 1))
                    for half in range(2):
                        wait(dve, x_hi, ab, 2 * n + half + 1)
                        wait(dve, x_used, ab, 2 * (n - 1) + half + 1)
                        dve.tensor_tensor(xl[:, half_x[half]], xraw[n % 2][:, half_x[half]],
                                          xh[:, half_x[half]].bitcast(F32), ALU.subtract).then_inc(x_lo.sem, 1)
                elif stage == "mix_weights":
                    if n == 0:
                        make_mix(dve, 0)
                    dve.wait_ge(set_hi, n + 1)
                    dve.wait_ge(mix_made[n], 1)
                    dve.tensor_tensor(flat_mix[1][:, half_mix[n]], made[:, half_mix[n]],
                                      flat_mix[0][:, half_mix[n]].bitcast(F32), ALU.subtract).then_inc(set_lo, 1)
                elif stage == "projections":
                    for w, cut in ((qkvw, raw_qkv), (outw, raw_out)):
                        high, low = (w[:, part].rearrange("p k n -> p (k n)") for part in range(2))
                        dve.wait_ge(set_hi, 3 if w is qkvw else 4)
                        dve.tensor_tensor(low, cut, high.bitcast(F32), ALU.subtract).then_inc(set_lo, 1)
                elif stage == "mix":
                    wait(dve, x_used, ab, 2 * (n + 1))
                    dve.tensor_copy(resid[:, n, :], bank_s[n % 2][:, 0:D]).then_inc(mixed_out.sem, 1)
                    dve.bn_stats(stats[:, n].rearrange("p h s -> p (h s)"), bank_s[n % 2][:, 0:D])\
                       .then_inc(mixed_out.sem, 1)
                elif stage == "ln1":
                    wait(dve, mixed_out, ab, 2 * TT)
                    norm_scale(ab)
                    if fb is None:
                        dve.wait_ge(consts_in, 16 * 9)
                    wait(dve, ln2_turned, ab, 0)
                    for t in range(TT):
                        dve.tensor_scalar(normed[:, t, :], resid[:, t, :], mean[:, t:t + 1], y1[:, t:t + 1],
                                          ALU.subtract, ALU.mult).then_inc(ln1_out.sem, 1)
                elif stage == "ln1_turn":
                    wait(dve, ln1_hi, ab, n + 1)
                    if n >= 2:
                        wait(dve, qkv_done, ab, n - 1)
                    dve.tensor_tensor(turned_l[:, n % 2], tile_ps[n % 2], turned_h[:, n % 2].bitcast(F32),
                                      ALU.subtract)\
                       .then_inc(ln1_lo.sem, 1)
                elif stage == "qkv":
                    wait(dve, qkv_done, ab, n + 1)
                    if n == 0:
                        wait(dve, weighed, ab, 0)
                    at_qk, at_v = qkv_banks(n, fb is None)
                    dve.tensor_tensor(qk[:, n, :], at_qk[:, :], qkvb[:, 0:2 * D], ALU.add).then_inc(qkv_out.sem, 1)
                    dve.tensor_tensor(v1[:, n, :, 0, :], at_v[:, 0:D].rearrange("p (h d) -> p h d", d=HD),
                                      qkvb[:, 2 * D:QKV].rearrange("p (h d) -> p h d", d=HD), ALU.add)\
                       .then_inc(qkv_out.sem, 1)
                elif stage == "rotate":
                    row = qk[:, n, :]
                    wait(dve, qkv_out, ab, 2 * n + 1)
                    pairs = row.rearrange("p (h f two) -> p h f two", f=HD // 2, two=2)
                    swapped = tmp_b[:].rearrange("p (h f two) -> p h f two", f=HD // 2, two=2)
                    sines = sin[:, n, :].rearrange("p (f two) -> p f two", two=2)
                    for side in range(2):
                        s = sines[:, :, side].unsqueeze(1).broadcast_to([P, 2 * HEADS, HD // 2])
                        ins = dve.tensor_tensor(swapped[:, :, :, side], pairs[:, :, :, 1 - side], s, ALU.mult)
                    att_v.link(dve, ins)
                    wait(dve, cosined, ab, n + 1)
                    wait(dve, squared, ab, n + 1)
                    dve.tensor_tensor(row, tmp_a[:], tmp_b[:], ALU.add)
                    dve.tensor_reduce(ss[:, n, :], squares.rearrange("p (h d) -> p h d", d=HD), AX.X, ALU.add)\
                       .then_inc(summed.sem, 1)
                elif stage == "qk_norm":
                    wait(dve, summed, ab, TT // 2 * (n + 1))
                    cut = slice(n * TT * HEADS, (n + 1) * TT * HEADS)
                    flat = ss[:].rearrange("p t h -> p (t h)")[:, cut]
                    att_v.link(dve, dve.tensor_scalar(flat, flat, NORM_EPS * NORM_EPS, None, ALU.max))
                    rsqrt(flat, cut)
                elif stage == "unit":
                    wait(dve, weighed, ab, 0)
                    scale = y1[:, n * 2 * HEADS:(n + 1) * 2 * HEADS].unsqueeze(2)\
                        .broadcast_to([P, 2 * HEADS, HD])
                    dve.tensor_tensor(units_at[:, n % 2, :].rearrange("p (h d) -> p h d", d=HD),
                                      qk[:, n, :].rearrange("p (h d) -> p h d", d=HD), scale, ALU.mult)\
                       .then_inc(qk_unit.sem, 1)
                elif stage == "stack":
                    wait(dve, qk_unit, ab, n + 1)
                    for a in range(2):
                        high, low, unit_qk = stack_slots(n, a)
                        wait(dve, stack_hi, ab, 2 * n + a + 1)
                        wait(dve, stack_turned, ab, 2 * (n - 1) + a + 1)
                        dve.tensor_tensor(low, unit_qk, high, ALU.subtract).then_inc(stack_ready.sem, 1)
                elif stage == "out_turn":
                    wait(dve, o_turned, ab, n + 1)
                    rows = bank_m[:, :].rearrange("p (t j d) -> p t j d", t=TT, j=4)
                    att_v.link(dve, dve.reciprocal(rc[:], rows[:, :, :, HD]))
                    if n == 0:
                        wait(dve, att_turned, ab, 0)
                    dve.tensor_tensor(att[:, :, n * 4 * HD:(n + 1) * 4 * HD].rearrange("p t (j d) -> p t j d", d=HD),
                                      rows[:, :, :, 0:HD], rc[:].unsqueeze(3).broadcast_to([P, TT, 4, HD]),
                                      ALU.mult).then_inc(att_out.sem, 1)
                elif stage == "att_turn":
                    wait(dve, att_hi, ab, n + 1)
                    if n >= 2:
                        wait(dve, projected, ab, n - 1)
                    dve.tensor_tensor(turned_l[:, n % 2], tile_ps[n % 2], turned_h[:, n % 2].bitcast(F32),
                                      ALU.subtract)\
                       .then_inc(att_lo.sem, 1)
                elif stage == "project":
                    wait(dve, projected, ab, n + 1)
                    wait(dve, resid_biased, ab, 1)
                    wait(dve, handed_acc, ab, 0)
                    ins = dve.tensor_tensor(accn[:, n, :], bank_s[n % 2][:, 0:D], resid[:, n, :], ALU.add)
                    ins.then_inc(h2_out.sem, 1)
                    wait(dve, h2_out, ab, n + 1)
                    att_v.link(dve, dve.bn_stats(stats[:, n].rearrange("p h s -> p (h s)"), accn[:, n, :]))
                elif stage == "ln2":
                    norm_scale(ab)
                    wait(dve, ln1_turned, ab, TT)
                    for t in range(TT):
                        dve.tensor_scalar(normed[:, t, :], accn[:, t, :], mean[:, t:t + 1], y1[:, t:t + 1],
                                          ALU.subtract, ALU.mult).then_inc(ln2_out.sem, 1)
                elif stage == "ln2_turn":
                    wait(dve, ln2_wide, ab, 2 * (n + 1))
                    cut = slice(n * P, (n + 1) * P)
                    dve.tensor_tensor(x16n[:, 1, :, cut], wide[:, n % 2], x16n[:, 0, :, cut], ALU.subtract)\
                       .then_inc(ln2_lo.sem, 1)
                elif stage == "gates":
                    wait(dve, gated, ab, TT)
                    dve.tensor_tensor(lg[:], bank_s[0][:, 0:TT * EXPERTS].rearrange("p (t e) -> p t e", t=TT),
                                      gateb[:].unsqueeze(1).broadcast_to([P, TT, EXPERTS]), ALU.add)\
                       .then_inc(logit.sem, 1)
                    wait(dve, gexp, ab, 1)
                    att_v.link(dve, dve.tensor_scalar(pg[:], eg[:], 1.0, None, ALU.add))
                    att_v.link(dve, dve.reciprocal(pg[:], pg[:]))
                    wait(dve, gturned, ab, 0)
                    flat = [z[:].rearrange("p t e -> p (t e)") for z in (wg, lg, pg)]
                    dve.scalar_tensor_tensor(flat[0], flat[1], 0.0, flat[2], ALU.is_gt, ALU.mult)\
                       .then_inc(gweight.sem, 1)
                    wait(dve, gweight, ab, 1)
                    dve.tensor_copy(gwn[:], wg[:]).then_inc(accn_ready.sem, 1)
                elif stage == "bias2":
                    wait(dve, b2_done, ab, 2)
                    for s in range(2):
                        cut = accn[:, 2 * s:2 * s + 2, :].rearrange("p t d -> p (t d)")
                        ins = dve.tensor_tensor(cut, bank_s[s][:, :], cut, ALU.add)
                    ins.then_inc(accn_ready.sem, 1)
                elif stage == "hand_x":
                    if fb is not None:
                        wait(dve, z_ready, fb, CHUNKS)
                    wait(dve, ln2_lo, ab, TT)
                    dve.tensor_copy(x16[:], x16n[:]).then_inc(handed_x.sem, 1)
                elif stage == "hand_acc":
                    wait(dve, stored, fb, 0)
                    wait(dve, acc_done, fb, 0)
                    wait(dve, accn_ready, fb, 2)
                    dve.tensor_copy(gw[:], gwn[:]).then_inc(handed_acc.sem, 1)
                    dve.tensor_copy(acc[:], accn[:]).then_inc(handed_acc.sem, 1)
                elif stage == "acc":
                    wait(dve, f2_done, fb, HM * (n + 1))
                    wait(dve, handed_acc, fb, 2)
                    wait(dve, acc_done, fb, TT * n)
                    dve.tensor_scalar(gs[:], gw[:, :, n], unscale[:, n:n + 1], None, ALU.mult)\
                       .then_inc(gate_unscaled.sem, 1)
                    wait(dve, gate_unscaled, fb, n + 1)
                    for t in range(TT):
                        dve.scalar_tensor_tensor(acc[:, t, :], bank_f[t // 2][:, t % 2 * D:(t % 2 + 1) * D],
                                                 gs[:, t:t + 1], acc[:, t, :], ALU.mult, ALU.add)\
                           .then_inc(acc_done.sem, 1)
                elif stage == "maxima":
                    e, second = divmod(n, 2)
                    dve.wait_ge(raw_in[second], 16 * (e + 1))
                    if e:
                        dve.wait_ge(maxima_all, e)
                    if not second:
                        dve.tensor_reduce(mx[:, 2:3], b1raw[:, e, :], AX.X, ALU.max, apply_absolute_value=True)\
                           .then_inc(maxima, 1)
                    dve.tensor_reduce(mx[:, second:second + 1], raw[:, 2048 * second:2048 * (second + 1)], AX.X,
                                      ALU.max, apply_absolute_value=True).then_inc(maxima, 1)
                elif stage == "scales":
                    make_scales(n)
                elif stage == "parts":
                    high, _, _ = piece(n, 0)
                    low, cut, scale = piece(n, 1)
                    if n < PIECES:
                        dve.tensor_scalar(high, cut, scale, None, ALU.mult).then_inc(parts_hi, 1)
                    dve.wait_ge(parts_hi, n + 1)
                    dve.scalar_tensor_tensor(low, cut, scale, high, ALU.mult, ALU.subtract).then_inc(parts_lo, 1)

            def make_scales(e):
                link = scale_v.link
                dve.wait_ge(maxima_all, e + 1)
                dve.scalar_tensor_tensor(bound[:, 0:1], mxr[:, 0:1], float(D), mxr[:, 2:3], ALU.mult, ALU.add)
                link(dve, dve.tensor_copy(bound[:, 1:2], mxr[:, 1:2]))
                link(dve, dve.tensor_scalar(bound[:], bound[:], FLOOR, None, ALU.max))
                link(dve, dve.tensor_scalar(pow2[:].bitcast(I32), bound[:].bitcast(I32), EXPONENT, None,
                                            ALU.bitwise_and))
                link(dve, dve.tensor_scalar(inv2[:].bitcast(I32), pow2[:].bitcast(I32), -1.0,
                                            float(2 * ONE_BITS), ALU.mult, ALU.add))
                if e:
                    dve.wait_ge(parts_hi, PIECES * e)
                link(dve, dve.tensor_scalar(scl[:], inv2[:], TOP, None, ALU.mult))
                link(dve, dve.scalar_tensor_tensor(unscale[:, e:e + 1], pow2[:, 0:1], TOP ** -2, pow2[:, 1:2],
                                                   ALU.mult, ALU.mult))
                dve.tensor_scalar(b1s[:, e, :], b1raw[:, e, :], scl[:, 0:1], None, ALU.mult).then_inc(scales, 1)

            run(dve, steps)


_OUTS = [((8, 512, 256), "float32")]


def _rope_tables(np):
    pos = np.arange(TOKENS, dtype=np.float32)
    half = HD // 2
    inv = (np.float32(1.0) / np.power(np.float32(2500), np.arange(half, dtype=np.float32) / np.float32(half)))
    theta = (pos[:, None] * inv.astype(np.float32)[None, :]).astype(np.float32)
    s, c = np.sin(theta), np.cos(theta)
    cos = np.repeat(c, 2, axis=1)
    sin = np.stack([-s, s], axis=-1).reshape(TOKENS, HD)
    return [np.ascontiguousarray(a.reshape(TT, P, HD).transpose(1, 0, 2)).astype(np.float32) for a in (cos, sin)]


def kernel(**inputs):
    import numpy as _np
    import concourse.bacc as _bacc
    from concourse import mybir as _mybir
    from concourse.bass_utils import run_bass_kernel_spmd as _run

    i = {k: _np.asarray(v) for k, v in inputs.items()}
    x_t = i["x"].reshape(BATCHES * TT, P, DK, P, TAPS).transpose(0, 3, 4, 2, 1).reshape(BATCHES * TT, P, XK, P)
    cos, sin = _rope_tables(_np)
    laid = {
        "x_t": x_t,
        "mix_w": i["L0_tok_weight"].T,
        "mix_sum_t": i["L0_tok_weighted_sum"].T,
        "qkv_w_t": i["L0_attn_qkv_w"].T,
        "qkv_b": i["L0_attn_qkv_b"],
        "out_w_t": i["L0_attn_out_w"].T,
        "out_b": i["L0_attn_out_b"],
        "gate_w": i["L0_ffn_Wg"],
        "gate_b": i["L0_ffn_bg"],
        "w1": i["L0_ffn_W1"],
        "b1_t": i["L0_ffn_b1"].reshape(EXPERTS, HM, P).transpose(2, 0, 1),
        "w2": i["L0_ffn_W2"],
        "b2": i["L0_ffn_b2"],
        "rope_cos": cos,
        "rope_sin": sin,
        "unit": _np.eye(P, dtype=_np.float32),
    }
    nc = _bacc.Bacc("TRN2", target_bir_lowering=False, num_devices=1)
    arrays, args = {}, []
    for name, a in laid.items():
        a = _np.ascontiguousarray(a)
        arrays[f"in_{name}_dram"] = a
        args.append(nc.dram_tensor(f"in_{name}_dram", a.shape, _mybir.dt.from_np(a.dtype), kind="ExternalInput").ap())
    for n, (shape, dtype) in enumerate(_OUTS):
        dt = _mybir.dt.from_np(_np.dtype(dtype))
        args.append(nc.dram_tensor(f"out_{n}_dram", shape, dt, kind="ExternalOutput").ap())
    build(nc, *args)
    r = _run(nc, [arrays], core_ids=[0])
    got = tuple(r.results[0][f"out_{n}_dram"] for n in range(len(_OUTS)))
    return got[0]
```
